# Optimizing a Trainium2 kernel written in Bass

```python
import numpy as np
import jax
import jax.numpy as jnp

def _softmax(x, axis=-1):
    return jax.nn.softmax(x, axis=axis)

def _gelu(x):
    return jax.nn.gelu(x, approximate=True)

def _silu(x):
    return jax.nn.silu(x)

def _sigmoid(x):
    return jax.nn.sigmoid(x)

def _layernorm(x, axis=-1, eps=1e-05):
    m = jnp.mean(x, axis=axis, keepdims=True)
    v = jnp.var(x, axis=axis, keepdims=True)
    return (x - m) / jnp.sqrt(v + eps)

def _scatter_add(tgt, idx, src, axis=0):
    return tgt.at[idx].add(src)

def _segment_sum(src, seg, n):
    return jax.ops.segment_sum(src, seg, n)
kernel_name = 'mk_decoder_preln_d1_seqx_r4_413597'

def setup_inputs(seed: int=0):
    np.random.seed(seed)
    _w = jnp.asarray

    def _rec_inputs():
        import jax
        import jax.numpy as jnp
        _rk = jax.random.key(seed)
        x = 4.136e-05 + 0.9999 * jax.random.normal(jax.random.fold_in(_rk, 1), (4, 512, 512), jnp.float32)
        _lenS = 512 - jax.random.randint(jax.random.fold_in(_rk, 7), (4,), 0, max(1, 512 // 4) + 1, jnp.int32)
        _lenS2 = 512 - jax.random.randint(jax.random.fold_in(_rk, 8), (4,), 0, max(1, 512 // 4) + 1, jnp.int32)
        _ctx_1024P = jax.random.normal(jax.random.fold_in(_rk, 11), (4, 16, 256), jnp.float32)
        _ctx_1024c = jax.random.dirichlet(jax.random.fold_in(_rk, 511), 0.3 * jnp.ones((16,), jnp.float32), (4, 512))
        _ctx_1024t = jnp.einsum('bsk,bkd->bsd', _ctx_1024c, _ctx_1024P)
        _ctx_1024t = _ctx_1024t * jax.lax.rsqrt(jnp.mean(jnp.square(_ctx_1024t)) + 1e-12) * 0.953939
        ctx_1024 = -0.000292821 + 1.00034 * (_ctx_1024t + 0.3 * jax.random.normal(jax.random.fold_in(_rk, 611), (4, 512, 256), jnp.float32))
        return (x, ctx_1024)
    x, ctx_1024 = _rec_inputs()

    def _L0_attn_setup():
        import jax, jax.numpy as jnp
        import numpy as np
        import math
        H = 512
        NH = 16
        HD = H // NH
        THETA = 10000.0

        def rotate_half(x):
            x1, x2 = (x[..., :HD // 2], x[..., HD // 2:])
            return jnp.concatenate((-x2, x1), axis=-1)

        def rope_tables(seq_len, dtype):
            inv_freq = 1.0 / THETA ** (np.arange(0, HD, 2, dtype=np.float32) / HD)
            t = np.arange(seq_len, dtype=np.float32)
            freqs = np.einsum('i,j->ij', t, inv_freq)
            emb = np.concatenate((freqs, freqs), axis=-1)
            return (jnp.asarray(np.cos(emb), dtype), jnp.asarray(np.sin(emb), dtype))
        key = jax.random.key(seed)
        ks = jax.random.split(key, 5)
        B, S = (2, 512)
        scale = 1.0 / math.sqrt(H)
        return {'hidden_states': jax.random.normal(ks[0], (B, S, H), jnp.float32), 'Wq': jax.random.normal(ks[1], (H, H), jnp.float32) * scale, 'Wk': jax.random.normal(ks[2], (H, H), jnp.float32) * scale, 'Wv': jax.random.normal(ks[3], (H, H), jnp.float32) * scale, 'Wo': jax.random.normal(ks[4], (H, H), jnp.float32) * scale}
    _L0_attn_all = _L0_attn_setup()
    _L0_attn_in = {k: v for k, v in _L0_attn_all.items() if k in ('Wq', 'Wk', 'Wv', 'Wo')}
    del _L0_attn_all

    def _L0_xattn_setup():
        import jax, jax.numpy as jnp
        import numpy as np
        import math
        B, L, DM = (2, 512, 256)
        DS, DC, EXP = (16, 4, 2)
        DI = EXP * DM
        DR = math.ceil(DM / 16)
        DT_MIN, DT_MAX, DT_FLOOR = (0.001, 0.1, 0.0001)

        def _ssm_forward(hidden_states, z, in_proj_w, conv_w, conv_b, x_proj_w, dt_proj_w, dt_proj_b, A_log, D):
            b = hidden_states.shape[0]
            x = jnp.einsum('ed,bld->bel', in_proj_w, hidden_states)
            xp = jnp.pad(x, ((0, 0), (0, 0), (DC - 1, 0)))
            xc = jax.lax.conv_general_dilated(xp, conv_w[:, None, :], window_strides=(1,), padding='VALID', dimension_numbers=('NCH', 'OIH', 'NCH'), feature_group_count=DI)
            u = jax.nn.silu(xc + conv_b[None, :, None])
            x_dbl = jnp.einsum('ke,bel->bkl', x_proj_w, u)
            dt_lo = x_dbl[:, :DR]
            Bm = x_dbl[:, DR:DR + DS]
            Cm = x_dbl[:, DR + DS:]
            delta = jax.nn.softplus(jnp.einsum('er,brl->bel', dt_proj_w, dt_lo) + dt_proj_b[None, :, None])
            A = -jnp.exp(A_log)

            def step(state, xs):
                d_t, B_t, C_t, u_t = xs
                dA = jnp.exp(d_t[..., None] * A)
                state = state * dA + (d_t * u_t)[..., None] * B_t[:, None, :]
                y_t = jnp.einsum('ben,bn->be', state, C_t)
                return (state, y_t)
            xs = (jnp.moveaxis(delta, -1, 0), jnp.moveaxis(Bm, -1, 0), jnp.moveaxis(Cm, -1, 0), jnp.moveaxis(u, -1, 0))
            state0 = jnp.zeros((b, DI, DS), delta.dtype)
            _, ys = jax.lax.scan(step, state0, xs)
            y = jnp.moveaxis(ys, 0, -1)
            y = y + D[None, :, None] * u
            y = y * jax.nn.silu(z)
            return jnp.swapaxes(y, 1, 2)
        key = jax.random.key(seed)
        ks = jax.random.split(key, 8)
        hidden_states = jax.random.normal(ks[0], (B, L, DM), jnp.float32)
        z = jax.random.normal(ks[1], (B, DI, L), jnp.float32)
        in_proj_w = jax.random.normal(ks[2], (DI, DM), jnp.float32) * DM ** (-0.5)
        conv_w = jax.random.normal(ks[3], (DI, DC), jnp.float32) * DC ** (-0.5)
        conv_b = jnp.zeros((DI,), jnp.float32)
        x_proj_w = jax.random.normal(ks[4], (DR + 2 * DS, DI), jnp.float32) * DI ** (-0.5)
        dt_std = DR ** (-0.5)
        dt_proj_w = jax.random.uniform(ks[5], (DI, DR), jnp.float32, -dt_std, dt_std)
        dt = jnp.exp(jax.random.uniform(ks[6], (DI,), jnp.float32) * (math.log(DT_MAX) - math.log(DT_MIN)) + math.log(DT_MIN))
        dt = jnp.clip(dt, DT_FLOOR)
        dt_proj_b = dt + jnp.log(-jnp.expm1(-dt))
        A_log = jnp.log(jnp.broadcast_to(jnp.arange(1, DS + 1, dtype=jnp.float32), (DI, DS)))
        D = jnp.ones((DI,), jnp.float32)
        return dict(hidden_states=hidden_states, z=z, in_proj_w=in_proj_w, conv_w=conv_w, conv_b=conv_b, x_proj_w=x_proj_w, dt_proj_w=dt_proj_w, dt_proj_b=dt_proj_b, A_log=A_log, D=D)
    _L0_xattn_all = _L0_xattn_setup()
    _L0_xattn_in = {k: v for k, v in _L0_xattn_all.items() if k in ('in_proj_w', 'conv_w', 'conv_b', 'x_proj_w', 'dt_proj_w', 'dt_proj_b', 'A_log', 'D')}
    del _L0_xattn_all

    def _L0_ffn_setup():
        import jax, jax.numpy as jnp
        import numpy as np
        H, I, E, TOP_K = (512, 352, 16, 6)
        IS = 704
        NORM_TOPK_PROB = False

        def _silu_and_mul(gate_up):
            d = gate_up.shape[-1] // 2
            g, u = (gate_up[..., :d], gate_up[..., d:])
            return jax.nn.silu(g) * u
        key = jax.random.key(seed)
        ks = jax.random.split(key, 6)
        s = 0.02
        return {'x': jax.random.normal(ks[0], (1, 512, H), jnp.float32), 'gate_w': jax.random.normal(ks[1], (E, H), jnp.float32) * s, 'w1': jax.random.normal(ks[2], (E, 2 * I, H), jnp.float32) * s, 'w2': jax.random.normal(ks[3], (E, H, I), jnp.float32) * s, 'shared_w1': jax.random.normal(ks[4], (2 * IS, H), jnp.float32) * s, 'shared_w2': jax.random.normal(ks[5], (H, IS), jnp.float32) * s}
    _L0_ffn_all = _L0_ffn_setup()
    _L0_ffn_in = {k: v for k, v in _L0_ffn_all.items() if k in ('gate_w', 'w1', 'w2', 'shared_w1', 'shared_w2')}
    del _L0_ffn_all
    return {'x': x, 'ctx_1024': ctx_1024, 'L0_attn_Wq': _L0_attn_in['Wq'], 'L0_attn_Wk': _L0_attn_in['Wk'], 'L0_attn_Wv': _L0_attn_in['Wv'], 'L0_attn_Wo': _L0_attn_in['Wo'], 'L0_xattn_in_proj_w': _L0_xattn_in['in_proj_w'], 'L0_xattn_conv_w': _L0_xattn_in['conv_w'], 'L0_xattn_conv_b': _L0_xattn_in['conv_b'], 'L0_xattn_x_proj_w': _L0_xattn_in['x_proj_w'], 'L0_xattn_dt_proj_w': _L0_xattn_in['dt_proj_w'], 'L0_xattn_dt_proj_b': _L0_xattn_in['dt_proj_b'], 'L0_xattn_A_log': _L0_xattn_in['A_log'], 'L0_xattn_D': _L0_xattn_in['D'], 'L0_ffn_gate_w': _L0_ffn_in['gate_w'], 'L0_ffn_w1': _L0_ffn_in['w1'], 'L0_ffn_w2': _L0_ffn_in['w2'], 'L0_ffn_shared_w1': _L0_ffn_in['shared_w1'], 'L0_ffn_shared_w2': _L0_ffn_in['shared_w2']}

def reference(x, ctx_1024, L0_attn_Wq, L0_attn_Wk, L0_attn_Wv, L0_attn_Wo, L0_xattn_in_proj_w, L0_xattn_conv_w, L0_xattn_conv_b, L0_xattn_x_proj_w, L0_xattn_dt_proj_w, L0_xattn_dt_proj_b, L0_xattn_A_log, L0_xattn_D, L0_ffn_gate_w, L0_ffn_w1, L0_ffn_w2, L0_ffn_shared_w1, L0_ffn_shared_w2):
    import jax
    import jax.numpy as jnp

    def _L0_attn_ref(hidden_states, Wq, Wk, Wv, Wo):
        import jax, jax.numpy as jnp
        import numpy as np
        import math
        H = 512
        NH = 16
        HD = H // NH
        THETA = 10000.0

        def rotate_half(x):
            x1, x2 = (x[..., :HD // 2], x[..., HD // 2:])
            return jnp.concatenate((-x2, x1), axis=-1)

        def rope_tables(seq_len, dtype):
            inv_freq = 1.0 / THETA ** (np.arange(0, HD, 2, dtype=np.float32) / HD)
            t = np.arange(seq_len, dtype=np.float32)
            freqs = np.einsum('i,j->ij', t, inv_freq)
            emb = np.concatenate((freqs, freqs), axis=-1)
            return (jnp.asarray(np.cos(emb), dtype), jnp.asarray(np.sin(emb), dtype))
        B, S, _ = hidden_states.shape

        def proj(W):
            y = jnp.einsum('bsh,oh->bso', hidden_states, W)
            return y.reshape(B, S, NH, HD).transpose(0, 2, 1, 3)
        q, k, v = (proj(Wq), proj(Wk), proj(Wv))
        cos, sin = rope_tables(S, hidden_states.dtype)
        cos, sin = (cos[None, None], sin[None, None])
        q = q * cos + rotate_half(q) * sin
        k = k * cos + rotate_half(k) * sin
        scores = jnp.einsum('bhqd,bhkd->bhqk', q, k) / math.sqrt(HD)
        causal = jnp.triu(jnp.ones((S, S), bool), k=1)
        scores = jnp.where(causal, -jnp.inf, scores)
        attn = jax.nn.softmax(scores, axis=-1)
        out = jnp.einsum('bhqk,bhkd->bhqd', attn, v)
        out = out.transpose(0, 2, 1, 3).reshape(B, S, H)
        return jnp.einsum('bsh,oh->bso', out, Wo)

    def _L0_xattn_ref(hidden_states, z, in_proj_w, conv_w, conv_b, x_proj_w, dt_proj_w, dt_proj_b, A_log, D):
        import jax, jax.numpy as jnp
        import numpy as np
        import math
        B, L, DM = (2, 512, 256)
        DS, DC, EXP = (16, 4, 2)
        DI = EXP * DM
        DR = math.ceil(DM / 16)
        DT_MIN, DT_MAX, DT_FLOOR = (0.001, 0.1, 0.0001)

        def _ssm_forward(hidden_states, z, in_proj_w, conv_w, conv_b, x_proj_w, dt_proj_w, dt_proj_b, A_log, D):
            b = hidden_states.shape[0]
            x = jnp.einsum('ed,bld->bel', in_proj_w, hidden_states)
            xp = jnp.pad(x, ((0, 0), (0, 0), (DC - 1, 0)))
            xc = jax.lax.conv_general_dilated(xp, conv_w[:, None, :], window_strides=(1,), padding='VALID', dimension_numbers=('NCH', 'OIH', 'NCH'), feature_group_count=DI)
            u = jax.nn.silu(xc + conv_b[None, :, None])
            x_dbl = jnp.einsum('ke,bel->bkl', x_proj_w, u)
            dt_lo = x_dbl[:, :DR]
            Bm = x_dbl[:, DR:DR + DS]
            Cm = x_dbl[:, DR + DS:]
            delta = jax.nn.softplus(jnp.einsum('er,brl->bel', dt_proj_w, dt_lo) + dt_proj_b[None, :, None])
            A = -jnp.exp(A_log)

            def step(state, xs):
                d_t, B_t, C_t, u_t = xs
                dA = jnp.exp(d_t[..., None] * A)
                state = state * dA + (d_t * u_t)[..., None] * B_t[:, None, :]
                y_t = jnp.einsum('ben,bn->be', state, C_t)
                return (state, y_t)
            xs = (jnp.moveaxis(delta, -1, 0), jnp.moveaxis(Bm, -1, 0), jnp.moveaxis(Cm, -1, 0), jnp.moveaxis(u, -1, 0))
            state0 = jnp.zeros((b, DI, DS), delta.dtype)
            _, ys = jax.lax.scan(step, state0, xs)
            y = jnp.moveaxis(ys, 0, -1)
            y = y + D[None, :, None] * u
            y = y * jax.nn.silu(z)
            return jnp.swapaxes(y, 1, 2)
        return _ssm_forward(hidden_states, z, in_proj_w, conv_w, conv_b, x_proj_w, dt_proj_w, dt_proj_b, A_log, D)

    def _L0_ffn_ref(x, gate_w, w1, w2, shared_w1, shared_w2):
        import jax, jax.numpy as jnp
        import numpy as np
        H, I, E, TOP_K = (512, 352, 16, 6)
        IS = 704
        NORM_TOPK_PROB = False

        def _silu_and_mul(gate_up):
            d = gate_up.shape[-1] // 2
            g, u = (gate_up[..., :d], gate_up[..., d:])
            return jax.nn.silu(g) * u
        B, S, Hd = x.shape
        xf = x.reshape(-1, Hd)
        T = xf.shape[0]
        shared_out = _silu_and_mul(xf @ shared_w1.T) @ shared_w2.T
        logits = xf @ gate_w.T
        probs = jax.nn.softmax(logits.astype(jnp.float32), axis=-1)
        routing_weights, selected = jax.lax.top_k(probs, TOP_K)
        if NORM_TOPK_PROB:
            routing_weights = routing_weights / routing_weights.sum(-1, keepdims=True)
        combine = jnp.zeros((T, E), jnp.float32).at[jnp.arange(T)[:, None], selected].add(routing_weights).astype(x.dtype)
        gate_up = jnp.einsum('th,eoh->teo', xf, w1)
        act = _silu_and_mul(gate_up)
        moe_out = jnp.einsum('te,tei,ehi->th', combine, act, w2)
        return (moe_out + shared_out).reshape(B, S, Hd)
    x = x + _L0_attn_ref(_layernorm(x, axis=-1), L0_attn_Wq, L0_attn_Wk, L0_attn_Wv, L0_attn_Wo)
    x = x + _L0_xattn_ref(ctx_1024, _layernorm(x, axis=-1), L0_xattn_in_proj_w, L0_xattn_conv_w, L0_xattn_conv_b, L0_xattn_x_proj_w, L0_xattn_dt_proj_w, L0_xattn_dt_proj_b, L0_xattn_A_log, L0_xattn_D)
    x = x + _L0_ffn_ref(_layernorm(x, axis=-1), L0_ffn_gate_w, L0_ffn_w1, L0_ffn_w2, L0_ffn_shared_w1, L0_ffn_shared_w2)
    return x

_drawn_inputs = setup_inputs


def setup_inputs(seed=0):
    import zlib

    import numpy as np

    out = dict(_drawn_inputs(seed))
    spreads = {'L0_xattn_conv_b': (0.0, 0.1), 'L0_xattn_D': (1.0, 0.2)}
    factors = {'L0_xattn_dt_proj_w': 5.298,
     'L0_ffn_gate_w': 7.636,
     'L0_ffn_w1': 6.076,
     'L0_ffn_w2': 6.081,
     'L0_ffn_shared_w1': 8.0,
     'L0_ffn_shared_w2': 8.0}
    for name, (base, spread) in spreads.items():
        noise = np.random.default_rng([zlib.crc32(name.encode()), seed]).standard_normal(out[name].shape)
        drawn = base * np.exp(spread * noise) if base else spread * noise
        out[name] = jnp.asarray(drawn.astype(out[name].dtype))
    for name, factor in factors.items():
        out[name] = (out[name] * factor).astype(out[name].dtype)
    return out
```

```python
from contextlib import ExitStack

import concourse.bass as bass
from concourse import mybir

F32 = mybir.dt.float32
F32R = mybir.dt.float32r
BF16 = mybir.dt.bfloat16
ALU = mybir.AluOpType
ACT = mybir.ActivationFunctionType
AX = mybir.AxisListType

P = 128
NB, S, H = 4, 512, 512
NT = S // P
NK = H // P
NH, HD = 16, 32
HG = P // HD
NG = NH // HG
SCALE = HD ** -0.5
EPS = 1e-5
DM, DI, DS, DC, DR = 256, 512, 16, 4, 16
NE = DI // P
NSG = DS // NG
STEPS = HG * NT
E, I, TOPK = 16, 352, 6
NX = E + 2
CH = [(0, 128), (128, 128), (256, 96)]
CST = 3 * P + 2 * S
PAR = 4 + 3 + DS


def build(nc, x_d, ctx_d, cst_d, par_d, wqkv_d, wo_d, inw_d, xpw_d, dtw_d, gate_d, w1_d, w2_d, bc_d, xt_d, out_d):
    sems = ExitStack()

    def sem(name):
        return sems.enter_context(nc.semaphore(name))

    with sems, ExitStack() as whole:
        def keep(name, shape, dt=F32):
            return whole.enter_context(nc.sbuf_tensor(name, shape, dt))

        acc = keep("acc", [P, NB * NT, H])
        comb = keep("comb", [P, NB * NT, NX])
        bank = [whole.enter_context(nc.psum_tensor(f"bank{i}", [P, 512], F32)) for i in range(8)]

        mixer_phase(nc, sem, bank, acc, comb, x_d, ctx_d, cst_d, par_d, wqkv_d, wo_d, inw_d, xpw_d,
                    dtw_d, gate_d, bc_d, xt_d)
        expert_phase(nc, sem, bank, acc, comb, xt_d, w1_d, w2_d, out_d)


def mixer_phase(nc, sem, bank, acc, comb, x_d, ctx_d, cst_d, par_d, wqkv_d, wo_d, inw_d, xpw_d,
                dtw_d, gate_d, bc_d, xt_d):
    with ExitStack() as st:
        def sb(name, shape, dt=F32):
            return st.enter_context(nc.sbuf_tensor(name, shape, dt))

        cst = sb("cst", [P, CST])
        ident, rot, mask = cst[:, 0:P], cst[:, P:2 * P], cst[:, 2 * P:3 * P]
        cos, sin = cst[:, 3 * P:3 * P + S], cst[:, 3 * P + S:CST]
        identb = sb("identb", [P, P], BF16)
        maskb = sb("maskb", [P, P], BF16)
        par = sb("par", [P, NE, PAR])
        conv_w = lambda e, k: par[:, e, k:k + 1]
        conv_b = lambda e: par[:, e, 4:5]
        dt_b = lambda e: par[:, e, 5:6]
        aneg = sb("aneg", [P, NE, DS])
        aexp = sb("aexp", [P, NE, DS])
        diagD = sb("diagD", [P, NE, P])
        wo = sb("wo", [P, NG, H])
        inw = sb("inw", [P, 2, DI])
        xpw = sb("xpw", [P, NE, DR + 2 * DS])
        dtw = sb("dtw", [DR, DI])
        gw = sb("gw", [P, NK, E])
        eps = sb("eps", [P, 1])

        xb = sb("xb", [P, NT, H])
        ctxT = sb("ctxT", [P, 2, S])
        ln = sb("ln", [P, NT, H])
        lnT = sb("lnT", [P, NK, S])
        nothing = sb("nothing", [P, 1])
        stats = sb("stats", [P, NT, 6])
        mv = sb("mv", [P, NT, 2])
        lnv = sb("lnv", [P, NT])
        r0 = sb("r0", [P, NT])
        nt1 = sb("nt1", [P, NT])
        nt2 = sb("nt2", [P, NT])
        nt3 = sb("nt3", [P, NT])
        rstd = sb("rstd", [P, NT])
        xin = sb("xin", [P, NE, S + DC - 1])
        u = sb("u", [P, NE, S])
        delta = sb("delta", [P, NE, S])
        du = sb("du", [P, NE, S])
        xdbl = sb("xdbl", [DR + 2 * DS, S])
        bcn = sb("bcn", [P, 2, 2, S])
        dA = sb("dA", [P, 2, S])
        dBu = sb("dBu", [P, 2, S])
        hst = sb("hst", [P, 2, S])
        hC = sb("hC", [P, 2, S])

        wqkv = sb("wqkv", [P, 3, NK, P])
        qraw = sb("qraw", [P, 2, S])
        qcos = sb("qcos", [P, 2, S])
        qsin = sb("qsin", [P, 2, S])
        qk = sb("qk", [P, 2, S])
        vg = sb("vg", [P, NT, P])
        prob = sb("prob", [P, 2, S])
        probT = sb("probT", [P, 2, S])
        mx = sb("mx", [P, STEPS])
        nmx = sb("nmx", [P, STEPS])
        rsum = sb("rsum", [P, STEPS])
        rinv = sb("rinv", [P, STEPS])
        rrep = sb("rrep", [P, NT, HG, HD])
        rbc = sb("rbc", [P, S])
        ao = sb("ao", [P, S])

        gmx = sb("gmx", [P, NT])
        gexp = sb("gexp", [P, NT, E])
        gsum = sb("gsum", [P, NT])
        grec = sb("grec", [P, NT])
        prb = sb("prb", [P, NT, E + 2])
        top8 = sb("top8", [P, NT, 8])
        rest = sb("rest", [P, NT, E + 2])

        Y = bank[0:4]
        S0, S1, TB, OB = bank[4:8]
        F4 = [S0, S1, TB, OB]

        s_const = sem("s_const")
        s_load = sem("s_load")
        s_wqkv = sem("s_wqkv")
        s_bcst = sem("s_bcst")
        s_bc = [sem(f"s_bc{i}") for i in range(2)]
        s_setup_a = sem("s_setup_a")
        s_setup_p = sem("s_setup_p")
        s_setup_v = sem("s_setup_v")
        s_var = sem("s_var")
        s_lnv = sem("s_lnv")
        s_r0 = sem("s_r0")
        s_ln = sem("s_ln")
        s_lnTp = sem("s_lnTp")
        s_lnT = sem("s_lnT")
        s_xinp = sem("s_xinp")
        s_xin = sem("s_xin")
        s_conv = sem("s_conv")
        s_tanh = sem("s_tanh")
        s_u = sem("s_u")
        s_xdp = sem("s_xdp")
        s_xd = sem("s_xd")
        s_dtp = sem("s_dtp")
        s_abs = sem("s_abs")
        s_relu = sem("s_relu")
        s_e = sem("s_e")
        s_l = sem("s_l")
        s_w1 = sem("s_w1")
        s_l2 = sem("s_l2")
        s_delta = sem("s_delta")
        s_du = sem("s_du")
        s_yinit = sem("s_yinit")
        s_qp = sem("s_qp")
        s_qraw = sem("s_qraw")
        s_v = sem("s_v")
        s_rotp = sem("s_rotp")
        s_qcos = sem("s_qcos")
        s_qsin = sem("s_qsin")
        s_qk = sem("s_qk")
        s_sc = sem("s_sc")
        s_mx = sem("s_mx")
        s_nmx = sem("s_nmx")
        s_prob = sem("s_prob")
        s_tp = sem("s_tp")
        s_pt = sem("s_pt")
        s_pv = sem("s_pv")
        s_dA = sem("s_dA")
        s_dBu = sem("s_dBu")
        s_scan = sem("s_scan")
        s_hC = sem("s_hC")
        s_y = sem("s_y")
        s_rinv = sem("s_rinv")
        s_rrep = sem("s_rrep")
        s_rbp = sem("s_rbp")
        s_rbc = sem("s_rbc")
        s_ao = sem("s_ao")
        s_wop = sem("s_wop")
        s_att = sem("s_att")
        s_th = sem("s_th")
        s_gz = sem("s_gz")
        s_yg = sem("s_yg")
        s_ytp = sem("s_ytp")
        s_x2 = sem("s_x2")
        s_xt = sem("s_xt")
        s_gp = sem("s_gp")
        s_gmx = sem("s_gmx")
        s_gexp = sem("s_gexp")
        s_gv = sem("s_gv")
        s_accst = sem("s_accst")
        s_small = sem("s_small")

        from_one = (s_accst, s_qp, s_qk, s_xt, s_bcst, s_tp, s_pv, s_y, s_gexp, s_yg, s_att)

        with nc.Block() as block:

            @block.sync
            def _(sp):
                for one in from_one:
                    sp.sem_inc(one, 1)
                for dst, src in ((cst[:, :], cst_d[:, :]), (par[:, :, :], par_d[:, :, :]), (wo[:, :, :], wo_d[:, :, :]),
                                 (inw[:, :, :], inw_d[:, :, :]), (xpw[:, :, :], xpw_d[:, :, :]),
                                 (dtw[:, :], dtw_d[:, :]), (gw[:, :, :], gate_d[:, :, :])):
                    sp.dma_start(dst, src).then_inc(s_const, 16)
                with sp.Fori(0, NB) as b:
                    sp.wait_ge(s_accst, 1 + b)
                    sp.dma_start(xb[:, :, :], x_d[bass.ds(b, 1), :, :, :].rearrange("a p t h -> (a p) t h")).then_inc(s_load, 16)
                    sp.dma_start(ctxT[:, :, :], ctx_d[bass.ds(b, 1), :, :, :].rearrange("a p t h -> (a p) t h")).then_inc(s_load, 16)
                    sp.wait_ge(s_xd, b + 1)
                    sp.dma_start(bc_d[bass.ds(b, 1), :, :].rearrange("a r s -> (a r) s"), xdbl[DR:DR + 2 * DS, :]).then_inc(s_bcst, 16)
                    with sp.Fori(0, NG) as g:
                        it = b * NG + g
                        sp.wait_ge(s_bcst, 1 + b * 16 + 16)
                        sp.wait_ge(s_qp, 1 + it * 3)
                        sp.dma_start(wqkv[:, :, :, :], wqkv_d[bass.ds(g, 1), :, :, :, :].rearrange("a p c k o -> (a p) c k o")).then_inc(s_wqkv, 16)
                        for n in range(NSG):
                            sp.wait_ge(s_hC, (it * NSG + n) * NE + NE)
                            for row in range(2):
                                src = bc_d[bass.ds(b, 1), bass.ds(g * NSG + (row * DS + n), 1), :].rearrange("a r s -> (a r) s")
                                sp.dma_start(bcn[:, n % 2, row, :], src.to_broadcast([P, S])).then_inc(s_bc[n % 2], 16)
                    sp.wait_ge(s_lnT, b * 2 * NK + 2 * NK)
                    sp.dma_start(xt_d[bass.ds(b, 1), :, :, :].rearrange("a p k s -> (a p) k s"), lnT[:, :, :]).then_inc(s_xt, 16)
                sp.wait_ge(s_xt, 1 + NB * 16)

            @block.gpsimd
            def _(pool):
                pool.memset(xin[:, :, 0:DC - 1], 0.0).then_inc(s_setup_p, 1)
                pool.memset(eps[:, :], EPS).then_inc(s_setup_p, 1)
                pool.memset(comb[:, :, E:NX], 1.0).then_inc(s_setup_p, 1)
                pool.memset(prb[:, :, E:E + 2], -1.0).then_inc(s_setup_p, 1)
                with pool.Fori(0, NB) as b:
                    for e in range(NE):
                        pool.wait_ge(s_w1, b * 2 * NE + NE + e + 1)
                        pool.wait_ge(s_l, b * NE + e + 1)
                        pool.tensor_tensor(ln[:, e, :], ln[:, e, :], xin[:, e, DC - 1:], ALU.subtract).then_inc(s_l2, 1)
                    for e in range(NE):
                        pool.wait_ge(s_l2, b * NE + e + 1)
                        pool.wait_ge(s_relu, b * NE + e + 1)
                        pool.tensor_tensor(delta[:, e, :], delta[:, e, :], ln[:, e, :], ALU.add).then_inc(s_delta, 1)
                    for e in range(NE):
                        pool.wait_ge(s_delta, b * NE + e + 1)
                        pool.tensor_tensor(du[:, e, :], delta[:, e, :], u[:, e, :], ALU.mult).then_inc(s_du, 1)
                    with pool.Fori(0, NG) as g:
                        it = b * NG + g
                        for c in range(2):
                            pool.wait_ge(s_qraw, it * 2 + c + 1)
                            pool.wait_ge(s_qk, 1 + it * 2)
                            pool.tensor_tensor(qcos[:, c, :], qraw[:, c, :], cos, ALU.mult).then_inc(s_qcos, 1)
                        for s in range(STEPS):
                            n, e = divmod(s, NE)
                            if s == 0:
                                pool.wait_ge(s_du, b * NE + NE)
                            if e == 0:
                                pool.wait_ge(s_bc[n % 2], it * (NSG // 2) * 32 + (n // 2) * 32 + 32)
                            pool.wait_ge(s_scan, it * STEPS + s + 1)
                            pool.tensor_tensor(dBu[:, s % 2, :], du[:, e, :], bcn[:, n % 2, 0, :], ALU.mult).then_inc(s_dBu, 1)

            @block.scalar
            def _(act):
                act.wait_ge(s_const, 16 * 7)
                act.wait_ge(s_setup_p, 4)
                act.activation(aexp[:, :, :], par[:, :, 7:PAR], ACT.Exp).then_inc(s_setup_a, 1)
                act.activation(identb[:, :], ident, ACT.Copy).then_inc(s_setup_a, 1)
                act.activation(maskb[:, :], mask, ACT.Copy).then_inc(s_setup_a, 1)

                def rstd_guess(i):
                    act.wait_ge(s_var, i + 1)
                    act.activation(lnv[:, :], mv[:, :, 1], ACT.Ln, bias=eps[:, 0:1]).then_inc(s_lnv, 1)
                    act.wait_ge(s_lnv, i + 1)
                    act.activation(r0[:, :], lnv[:, :], ACT.Exp, scale=-0.5).then_inc(s_r0, 1)

                def copy_lnT(i):
                    for k in range(NK):
                        act.wait_ge(s_lnTp, i * NK + k + 1)
                        act.activation(lnT[:, k, :], F4[k][:, :], ACT.Copy).then_inc(s_lnT, 1)

                with act.Fori(0, NB) as b:
                    rstd_guess(b * 3)
                    act.wait_ge(s_xt, 1 + b * 16)
                    copy_lnT(b * 2)
                    for e in range(NE):
                        act.wait_ge(s_xinp, b * NE + e + 1)
                        act.activation(xin[:, e, DC - 1:], F4[e][:, :], ACT.Copy).then_inc(s_xin, 1)
                    for e in range(NE):
                        act.wait_ge(s_conv, b * NE * DC + NE * (DC - 1) + e + 1)
                        act.activation(delta[:, e, :], du[:, e, :], ACT.Tanh, scale=0.5).then_inc(s_tanh, 1)
                    act.wait_ge(s_xdp, b + 1)
                    act.wait_ge(s_bcst, 1 + b * 16)
                    act.activation(xdbl[:, :], S0[0:DR + 2 * DS, :], ACT.Copy).then_inc(s_xd, 1)
                    for e in range(NE):
                        act.wait_ge(s_dtp, b * NE + e + 1)
                        act.activation(ln[:, e, :], F4[e][:, :], ACT.Abs, bias=dt_b(e)).then_inc(s_abs, 1)
                    for e in range(NE):
                        act.wait_ge(s_abs, b * NE + e + 1)
                        act.activation(du[:, e, :], ln[:, e, :], ACT.Exp, scale=-1.0).then_inc(s_e, 1)
                    for e in range(NE):
                        act.wait_ge(s_e, b * NE + e + 1)
                        act.activation(ln[:, e, :], du[:, e, :], ACT.Ln, bias=1.0).then_inc(s_l, 1)

                    with act.Fori(0, NG) as g:
                        it = b * NG + g
                        for c, src in ((0, S0), (1, S1)):
                            act.wait_ge(s_qp, 1 + it * 3 + c + 1)
                            act.activation(qraw[:, c, :], src[:, :], ACT.Copy).then_inc(s_qraw, 1)
                        act.wait_ge(s_qp, 1 + it * 3 + 3)
                        act.activation(vg[:, :, :], TB[:, :].rearrange("p (t o) -> p t o", t=NT), ACT.Copy).then_inc(s_v, 1)

                        def decay(s):
                            n, e = divmod(s, NE)
                            if s == 0:
                                act.wait_ge(s_delta, b * NE + NE)
                            act.wait_ge(s_scan, it * STEPS + s + 1)
                            act.activation(dA[:, s % 2, :], delta[:, e, :], ACT.Exp,
                                           scale=aneg[:, e, bass.ds(g * NSG + n, 1)]).then_inc(s_dA, 1)

                        def softmax(s):
                            w = (s % NT + 1) * P
                            act.wait_ge(s_nmx, it * STEPS + s + 1)
                            act.wait_ge(s_tp, 1 + it * STEPS + max(s - 1, 0))
                            act.activation(prob[:, s % 2, 0:w], [S0, S1][s % 2][:, 0:w], ACT.Exp, bias=nmx[:, s:s + 1],
                                           scale=SCALE, accum_out=rsum[:, s:s + 1]).then_inc(s_prob, 1)

                        def copy_probT(s):
                            w = (s % NT + 1) * P
                            act.wait_ge(s_tp, 1 + it * STEPS + s + 1)
                            act.wait_ge(s_pv, 1 + it * STEPS + max(s - 1, 0))
                            act.activation(probT[:, s % 2, 0:w], TB[:, 0:w], ACT.Copy).then_inc(s_pt, 1)

                        decay(0)
                        for k in range(STEPS + 1):
                            if k + 1 < STEPS:
                                decay(k + 1)
                            if k < STEPS:
                                softmax(k)
                            if k >= 1:
                                copy_probT(k - 1)
                        act.wait_ge(s_rbp, it + 1)
                        act.activation(rbc[:, :], S0[:, :], ACT.Copy).then_inc(s_rbc, 1)

                    rstd_guess(b * 3 + 1)
                    for t in range(NT):
                        act.wait_ge(s_ln, b * 3 * NT + NT + t + 1)
                        act.activation(delta[:, t, :], ln[:, t, :], ACT.Tanh, scale=0.5).then_inc(s_th, 1)
                    rstd_guess(b * 3 + 2)
                    copy_lnT(b * 2 + 1)
                    for t in range(NT):
                        act.wait_ge(s_gmx, b + 1)
                        act.activation(gexp[:, t, :], OB[:, t * E:(t + 1) * E], ACT.Exp, bias=gmx[:, t:t + 1],
                                       accum_out=gsum[:, t:t + 1]).then_inc(s_gexp, 1)
                    act.activation(acc[:, bass.ds(b * NT, NT), :], xb[:, :, :], ACT.Copy).then_inc(s_accst, 1)

            @block.vector
            def _(v):
                v.wait_ge(s_const, 16 * 7)
                v.wait_ge(s_setup_a, 3)
                v.tensor_scalar(aneg[:, :, :], aexp[:, :, :], -1.0, None, ALU.mult).then_inc(s_setup_v, 1)
                for e in range(NE):
                    v.tensor_scalar(diagD[:, e, :], ident, par[:, e, 6:7], None, ALU.mult).then_inc(s_setup_v, 1)
                v.sem_inc(s_scan, 2)
                v.sem_inc(s_hC, 2 * NE)

                class Chain:
                    n = 0
                    base = 0

                def link(ins, own_wait=False):
                    Chain.n += 1
                    ins.then_inc(s_small, 1)
                    v.wait_ge(s_small, Chain.base + Chain.n)
                    if own_wait:
                        v.memset(nothing[:, :], 0.0)

                def layer_norm(i):
                    for t in range(NT):
                        ins = v.bn_stats(stats[:, t, :], xb[:, t, :])
                    link(ins, own_wait=True)
                    for t in range(NT):
                        ins = v.bn_aggr(mv[:, t, :], stats[:, t, :])
                    ins.then_inc(s_var, 1)
                    v.wait_ge(s_r0, i + 1)
                    link(v.tensor_tensor(nt1[:, :], r0[:, :], r0[:, :], ALU.mult))
                    link(v.scalar_tensor_tensor(nt2[:, :], mv[:, :, 1], EPS, nt1[:, :], ALU.add, ALU.mult))
                    link(v.tensor_scalar(nt3[:, :], nt2[:, :], -0.5, 1.5, ALU.mult, ALU.add))
                    link(v.tensor_tensor(rstd[:, :], r0[:, :], nt3[:, :], ALU.mult))
                    for t in range(NT):
                        v.tensor_scalar(ln[:, t, :], xb[:, t, :], mv[:, t, 0:1], rstd[:, t:t + 1], ALU.subtract,
                                        ALU.mult).then_inc(s_ln, 1)

                LINKS = 3 * 5 + 2 + 3 * NT
                with v.Fori(0, NB) as b:
                    Chain.n, Chain.base = 0, b * LINKS
                    v.wait_ge(s_load, b * 32 + 32)
                    layer_norm(b * 3)
                    for k in range(DC):
                        for e in range(NE):
                            n = b * NE * DC + NE * k + e
                            if k == 0:
                                v.wait_ge(s_xin, b * NE + e + 1)
                                v.tensor_scalar(du[:, e, :], xin[:, e, 0:S], conv_w(e, 0), conv_b(e), ALU.mult,
                                                ALU.add).then_inc(s_conv, 1)
                            else:
                                v.wait_ge(s_conv, n - NE + 1)
                                v.scalar_tensor_tensor(du[:, e, :], xin[:, e, k:k + S], conv_w(e, k), du[:, e, :],
                                                       ALU.mult, ALU.add).then_inc(s_conv, 1)
                    for e in range(NE):
                        v.wait_ge(s_tanh, b * NE + e + 1)
                        v.scalar_tensor_tensor(u[:, e, :], delta[:, e, :], 1.0, du[:, e, :], ALU.add,
                                               ALU.mult).then_inc(s_u, 1)
                    for e in range(NE):
                        v.wait_ge(s_u, b * 2 * NE + e + 1)
                        v.tensor_scalar(u[:, e, :], u[:, e, :], 0.5, None, ALU.mult).then_inc(s_u, 1)
                    for e in range(NE):
                        v.wait_ge(s_abs, b * NE + NE)
                        v.tensor_scalar(delta[:, e, :], F4[e][:, :], dt_b(e), 0.0, ALU.add, ALU.max).then_inc(s_relu, 1)
                    for e in range(NE):
                        v.wait_ge(s_e, b * NE + e + 1)
                        v.tensor_scalar(xin[:, e, DC - 1:], du[:, e, :], 1.0, 1.0, ALU.add, ALU.subtract).then_inc(s_w1, 1)
                    for e in range(NE):
                        v.wait_ge(s_w1, b * 2 * NE + e + 1)
                        v.tensor_tensor(xin[:, e, DC - 1:], xin[:, e, DC - 1:], du[:, e, :], ALU.subtract).then_inc(s_w1, 1)

                    with v.Fori(0, NG) as g:
                        it = b * NG + g
                        for c, src in ((0, OB), (1, S0)):
                            v.wait_ge(s_rotp, it * 2 + c + 1)
                            v.tensor_tensor(qsin[:, c, :], src[:, :], sin, ALU.mult).then_inc(s_qsin, 1)
                        for c in range(2):
                            v.wait_ge(s_qsin, it * 2 + c + 1)
                            v.wait_ge(s_qcos, it * 2 + c + 1)
                            v.tensor_tensor(qk[:, c, :], qcos[:, c, :], qsin[:, c, :], ALU.add).then_inc(s_qk, 1)

                        def c_product(s):
                            n = s // NE
                            v.wait_ge(s_scan, it * STEPS + s + 3)
                            v.wait_ge(s_y, 1 + it * STEPS + max(s - 1, 0))
                            v.tensor_tensor(hC[:, s % 2, :], hst[:, s % 2, :], bcn[:, n % 2, 1, :], ALU.mult).then_inc(s_hC, 1)

                        for s in range(STEPS):
                            w = (s % NT + 1) * P
                            v.wait_ge(s_sc, it * STEPS + s + 1)
                            v.tensor_reduce(mx[:, s:s + 1], [S0, S1][s % 2][:, 0:w], AX.X, ALU.max).then_inc(s_mx, 1)
                            v.wait_ge(s_dA, it * STEPS + s + 1)
                            v.wait_ge(s_dBu, it * STEPS + s + 1)
                            v.tensor_tensor_scan(hst[:, s % 2, :], dA[:, s % 2, :], dBu[:, s % 2, :], 0.0, ALU.mult,
                                                 ALU.add).then_inc(s_scan, 1)
                            v.wait_ge(s_mx, it * STEPS + s + 1)
                            v.tensor_scalar(nmx[:, s:s + 1], mx[:, s:s + 1], -SCALE, None, ALU.mult).then_inc(s_nmx, 1)
                            if s >= 1:
                                c_product(s - 1)
                        c_product(STEPS - 1)

                        v.wait_ge(s_prob, it * STEPS + STEPS)
                        v.reciprocal(rinv[:, :], rsum[:, :]).then_inc(s_rinv, 1)
                        v.wait_ge(s_rinv, it + 1)
                        v.tensor_copy(rrep[:, :, :, :],
                                      rinv[:, :].rearrange("p (j t) -> p t j", t=NT).unsqueeze(3).to_broadcast([P, NT, HG, HD])
                                      ).then_inc(s_rrep, 1)
                        v.wait_ge(s_rbc, it + 1)
                        v.wait_ge(s_pv, 1 + it * STEPS + STEPS)
                        v.tensor_tensor(ao[:, :], OB[:, :], rbc[:, :], ALU.mult).then_inc(s_ao, 1)
                        for t in range(NT):
                            v.wait_ge(s_wop, it * NT + t + 1)
                            v.tensor_tensor(xb[:, t, :], F4[t][:, :], xb[:, t, :], ALU.add).then_inc(s_att, 1)

                    v.wait_ge(s_att, 1 + b * NG * NT + NG * NT)
                    layer_norm(b * 3 + 1)
                    for t in range(NT):
                        v.wait_ge(s_th, b * NT + t + 1)
                        v.scalar_tensor_tensor(ln[:, t, :], delta[:, t, :], 1.0, ln[:, t, :], ALU.add,
                                               ALU.mult).then_inc(s_gz, 1)
                    for t in range(NT):
                        v.wait_ge(s_gz, b * NT + t + 1)
                        v.wait_ge(s_y, 1 + (b * NG + NG) * STEPS)
                        v.scalar_tensor_tensor(u[:, t, :], ln[:, t, :], 0.5, Y[t][:, :], ALU.mult,
                                               ALU.mult).then_inc(s_yg, 1)
                    for t in range(NT):
                        v.wait_ge(s_ytp, b * NT + t + 1)
                        v.tensor_tensor(xb[:, t, :], F4[t][:, :], xb[:, t, :], ALU.add).then_inc(s_x2, 1)
                    v.wait_ge(s_x2, b * NT + NT)
                    layer_norm(b * 3 + 2)
                    v.wait_ge(s_gp, b * NT + NT)
                    v.tensor_reduce(gmx[:, :], OB[:, 0:NT * E].rearrange("p (t e) -> p t e", t=NT), AX.X, ALU.max,
                                    negate=True).then_inc(s_gmx, 1)
                    v.wait_ge(s_gexp, 1 + b * NT + NT)
                    link(v.reciprocal(grec[:, :], gsum[:, :]))
                    for t in range(NT):
                        ins = v.tensor_scalar(prb[:, t, 0:E], gexp[:, t, :], grec[:, t:t + 1], None, ALU.mult)
                    link(ins, own_wait=True)
                    for t in range(NT):
                        link(v.max(top8[:, t, :], prb[:, t, 0:E]))
                        link(v.memset(top8[:, t, TOPK:8], -1.0), own_wait=True)
                        link(v.match_replace(rest[:, t, :], top8[:, t, :], prb[:, t, :], 0.0))
                        v.tensor_tensor(comb[:, bass.ds(b * NT + t, 1), 0:E].rearrange("p a e -> p (a e)"), prb[:, t, 0:E],
                                        rest[:, t, 0:E], ALU.subtract).then_inc(s_gv, 1)
                    assert Chain.n == LINKS, Chain.n

            @block.tensor
            def _(pe):
                pe.wait_ge(s_const, 16 * 7)
                pe.wait_ge(s_setup_v, 1 + NE)

                def transpose_ln(b, which):
                    for k in range(NK):
                        for t in range(NT):
                            if k == 0:
                                pe.wait_ge(s_ln, b * 3 * NT + which * NT + t + 1)
                            ins = pe.transpose(F4[k][:, t * P:(t + 1) * P], ln[:, t, k * P:(k + 1) * P], ident)
                        ins.then_inc(s_lnTp, 1)

                with pe.Fori(0, NB) as b:
                    pe.wait_ge(s_gexp, 1 + b * NT)
                    transpose_ln(b, 0)
                    for e in range(NE):
                        pe.wait_ge(s_lnT, b * 2 * NK + e + 1)
                        pe.wait_ge(s_load, b * 32 + 32)
                        for k in range(2):
                            ins = pe.matmul(F4[e][:, :], inw[:, k, e * P:(e + 1) * P], ctxT[:, k, :], start=(k == 0),
                                            stop=(k == 1))
                        ins.then_inc(s_xinp, 1)
                    pe.wait_ge(s_xin, b * NE + 1)
                    for e in range(NE):
                        pe.wait_ge(s_u, b * 2 * NE + NE + e + 1)
                        ins = pe.matmul(S0[0:DR + 2 * DS, :], xpw[:, e, :], u[:, e, :], start=(e == 0), stop=(e == NE - 1))
                    ins.then_inc(s_xdp, 1)
                    for e in range(NE):
                        pe.wait_ge(s_yg, 1 + b * NT)
                        ins = pe.matmul(Y[e][:, :], diagD[:, e, :], u[:, e, :], start=True, stop=False, skip_group_check=True)
                    ins.then_inc(s_yinit, 1)
                    pe.wait_ge(s_xd, b + 1)
                    pe.wait_ge(s_xin, b * NE + NE)
                    for e in range(NE):
                        pe.matmul(F4[e][:, :], dtw[:, e * P:(e + 1) * P], xdbl[0:DR, :], start=True, stop=True).then_inc(s_dtp, 1)

                    with pe.Fori(0, NG) as g:
                        it = b * NG + g
                        pe.wait_ge(s_relu, b * NE + NE)
                        pe.wait_ge(s_lnT, b * 2 * NK + NK)
                        pe.wait_ge(s_wqkv, it * 16 + 16)
                        pe.wait_ge(s_att, 1 + it * NT)
                        for c, dst in ((0, S0), (1, S1)):
                            for k in range(NK):
                                ins = pe.matmul(dst[:, :], wqkv[:, c, k, :], lnT[:, k, :], start=(k == 0), stop=(k == NK - 1))
                            ins.then_inc(s_qp, 1)
                        for t in range(NT):
                            for k in range(NK):
                                ins = pe.matmul(TB[:, t * P:(t + 1) * P], lnT[:, k, t * P:(t + 1) * P], wqkv[:, 2, k, :],
                                                start=(k == 0), stop=(k == NK - 1))
                        ins.then_inc(s_qp, 1)
                        for c, dst in ((0, OB), (1, S0)):
                            pe.wait_ge(s_qraw, it * 2 + c + 1)
                            pe.matmul(dst[:, :], rot, qraw[:, c, :], start=True, stop=True).then_inc(s_rotp, 1)

                        def scores(s):
                            j, t = divmod(s, NT)
                            r = slice(j * HD, (j + 1) * HD)
                            if s == 0:
                                pe.wait_ge(s_qk, 1 + it * 2 + 2)
                                pe.wait_ge(s_qsin, it * 2 + 2)
                            if s >= 2:
                                pe.wait_ge(s_prob, it * STEPS + s - 1)
                            dst = [S0, S1][s % 2]
                            w = (t + 1) * P
                            pe.matmul(dst[:, 0:w], qk[r, 0, t * P:w], qk[r, 1, 0:w], start=True, stop=False)
                            pe.matmul(dst[:, t * P:w], identb[:, :], maskb[:, :], start=False, stop=True).then_inc(s_sc, 1)

                        def transposes(s):
                            t = s % NT
                            pe.wait_ge(s_prob, it * STEPS + s + 1)
                            if s == 0:
                                pe.wait_ge(s_v, it + 1)
                            else:
                                pe.wait_ge(s_pt, it * STEPS + s)
                            for k in range(t + 1):
                                ins = pe.transpose(TB[:, k * P:(k + 1) * P], prob[:, s % 2, k * P:(k + 1) * P], ident)
                            ins.then_inc(s_tp, 1)

                        def values(s):
                            j, t = divmod(s, NT)
                            pe.wait_ge(s_pt, it * STEPS + s + 1)
                            for k in range(t + 1):
                                ins = pe.matmul(OB[j * HD:(j + 1) * HD, t * P:(t + 1) * P], vg[:, k, j * HD:(j + 1) * HD],
                                                probT[:, s % 2, k * P:(k + 1) * P], start=(k == 0), stop=(k == t))
                            ins.then_inc(s_pv, 1)

                        def sum_states(s):
                            e = s % NE
                            pe.wait_ge(s_hC, it * STEPS + s + 1 + 2 * NE)
                            pe.matmul(Y[e][:, :], ident, hC[:, s % 2, :], start=False, stop=False,
                                      skip_group_check=True).then_inc(s_y, 1)

                        for k in range(STEPS + 2):
                            if k < STEPS:
                                scores(k)
                            if 1 <= k <= STEPS:
                                transposes(k - 1)
                            if k >= 2:
                                values(k - 2)
                            if 1 <= k <= STEPS:
                                sum_states(k - 1)
                        pe.wait_ge(s_rrep, it + 1)
                        for t in range(NT):
                            ins = pe.matmul(S0[:, t * P:(t + 1) * P], rrep[:, t, :, :].rearrange("p j d -> p (j d)"), ident,
                                            start=True, stop=True)
                        ins.then_inc(s_rbp, 1)
                        pe.wait_ge(s_ao, it + 1)
                        for t in range(NT):
                            pe.matmul(F4[t][:, :], ao[:, t * P:(t + 1) * P], wo[:, bass.ds(g, 1), :].rearrange("p a h -> p (a h)"),
                                      start=True, stop=True).then_inc(s_wop, 1)

                    pe.wait_ge(s_att, 1 + (b * NG + NG) * NT)
                    for t in range(NT):
                        for e in range(NE):
                            pe.wait_ge(s_yg, 1 + b * NT + e + 1)
                            ins = pe.transpose(F4[t][:, e * P:(e + 1) * P], u[:, e, t * P:(t + 1) * P], ident)
                        ins.then_inc(s_ytp, 1)
                    pe.wait_ge(s_x2, b * NT + NT)
                    transpose_ln(b, 2)
                    pe.wait_ge(s_lnT, b * 2 * NK + 2 * NK)
                    for t in range(NT):
                        for k in range(NK):
                            ins = pe.matmul(OB[:, t * E:(t + 1) * E], lnT[:, k, t * P:(t + 1) * P], gw[:, k, :],
                                            start=(k == 0), stop=(k == NK - 1))
                        ins.then_inc(s_gp, 1)


def expert_phase(nc, sem, bank, acc, comb, xt_d, w1_d, w2_d, out_d):
    with ExitStack() as st:
        def sb(name, shape, dt=F32):
            return st.enter_context(nc.sbuf_tensor(name, shape, dt))

        xTh = sb("xTh", [P, NK, NB * S], F32R)
        xTl = sb("xTl", [P, NK, NB * S], F32R)
        NQ = NB
        raw1 = sb("raw1", [P, NK, 2 * I])
        raw2 = sb("raw2", [P, 3, H])
        w1h = [sb(f"w1h{i}", [P, NK, 2 * I], F32R) for i in range(2)]
        w1l = [sb(f"w1l{i}", [P, NK, 2 * I], F32R) for i in range(2)]
        w2h = [sb(f"w2h{i}", [P, 3, H], F32R) for i in range(2)]
        w2l = [sb(f"w2l{i}", [P, 3, H], F32R) for i in range(2)]
        silu = sb("silu", [P, S])
        a = sb("a", [P, 3, S])
        ah = sb("ah", [P, 3, S], F32R)
        al = sb("al", [P, 3, S], F32R)
        GATE, UP = [bank[0], bank[2], bank[4]], [bank[1], bank[3], bank[5]]
        DOWN = bank[6:8]

        s_zero = sem("s_zero")
        s_x = sem("s_x")
        s_xh = sem("s_xh")
        s_xl = sem("s_xl")
        s_raw = sem("s_raw")
        s_hi = sem("s_whi")
        s_lo = sem("s_wlo")
        s_up = sem("s_up")
        s_silu = sem("s_silu")
        s_a = sem("s_a")
        s_ah = sem("s_ah")
        s_al = sem("s_al")
        s_dn = sem("s_dn")
        s_acc = sem("s_acc")
        s_out = sem("s_out")
        PAIRS = NX // 2

        def rows(c):
            return CH[c][1]

        def each_expert(eng, body):
            with eng.Fori(0, PAIRS - 1) as pr:
                body(pr * 2, 0, True)
                body(pr * 2 + 1, 1, True)
            body(NX - 2, 0, True)
            body(NX - 1, 1, False)

        from_one = (s_lo, s_hi, s_a, s_dn, s_ah, s_acc)

        with nc.Block() as block:

            @block.sync
            def _(sp):
                for one in from_one:
                    sp.sem_inc(one, 1)
                for q in range(NQ):
                    sp.dma_start(xTl[:, :, q * S:(q + 1) * S].bitcast(F32), xt_d[q]).then_inc(s_x, 16)
                sp.wait_ge(s_zero, 1)
                with sp.Fori(0, NX) as x:
                    sp.wait_ge(s_lo, 1 + x * NQ)
                    sp.wait_ge(s_hi, 1 + x * NQ)
                    sp.dma_start(raw1[:, :, :], w1_d[bass.ds(x, 1), :, :, :].rearrange("a p k o -> (a p) k o")).then_inc(s_raw, 16)
                    w2x = w2_d[bass.ds(x, 1), :, :].rearrange("a i h -> (a i) h")
                    sp.dma_start(raw2[:, 0:2, :], w2x[0:2 * P, :].rearrange("(c p) h -> p c h", p=P)).then_inc(s_raw, 16)
                    sp.dma_start(raw2[0:I - 2 * P, 2, :], w2x[2 * P:I, :]).then_inc(s_raw, 16)
                sp.wait_ge(s_acc, 1 + NX * NQ * NT)
                sp.dma_start(out_d[:, :, :], acc[:, :, :]).then_inc(s_out, 16)
                sp.wait_ge(s_out, 16)

            @block.scalar
            def _(act):
                def split_hi(x, par, q):
                    act.wait_ge(s_raw, x * 48 + 48)
                    act.activation(w1h[par][:, bass.ds(q, 1), :], raw1[:, bass.ds(q, 1), :], ACT.Copy)
                    act.activation(w2h[par][:, :, bass.ds(q * P, P)], raw2[:, :, bass.ds(q * P, P)], ACT.Copy).then_inc(s_hi, 1)

                def body(x, par, nxt):
                    with act.Fori(0, NQ) as q:
                        n = x * NQ + q
                        for c in range(3):
                            m = rows(c)
                            act.wait_ge(s_up, n * 3 + c + 1)
                            act.wait_ge(s_a, 1 + n * 3 + c)
                            act.activation(silu[0:m, :], GATE[c][0:m, :], ACT.Silu).then_inc(s_silu, 1)
                            if c == 0 and nxt:
                                act.wait_ge(s_dn, 1 + x * NQ * NT)
                                split_hi(x + 1, 1 - par, q)
                            act.wait_ge(s_a, 1 + n * 3 + c + 1)
                            act.wait_ge(s_dn, 1 + n * NT)
                            act.activation(ah[0:m, c, :], a[0:m, c, :], ACT.Copy).then_inc(s_ah, 1)

                with act.Fori(0, NQ) as q:
                    split_hi(0, 0, q)
                for q in range(NQ):
                    act.wait_ge(s_x, NQ * 16)
                    tok = slice(q * S, (q + 1) * S)
                    act.activation(xTh[:, :, tok], xTl[:, :, tok].bitcast(F32), ACT.Copy).then_inc(s_xh, 1)
                each_expert(act, body)

            @block.gpsimd
            def _(pool):
                pool.memset(raw2[:, 2, :], 0.0).then_inc(s_zero, 1)

                def split_lo(x, par, q):
                    pool.wait_ge(s_hi, 1 + x * NQ + q + 1)
                    sl = bass.ds(q * P, P)
                    pool.tensor_tensor(w1l[par][:, bass.ds(q, 1), :], raw1[:, bass.ds(q, 1), :],
                                       w1h[par][:, bass.ds(q, 1), :].bitcast(F32), ALU.subtract)
                    pool.tensor_tensor(w2l[par][:, :, sl], raw2[:, :, sl], w2h[par][:, :, sl].bitcast(F32),
                                       ALU.subtract).then_inc(s_lo, 1)

                def body(x, par, nxt):
                    if nxt:
                        with pool.Fori(0, NQ) as q:
                            split_lo(x + 1, 1 - par, q)

                with pool.Fori(0, NQ) as q:
                    split_lo(0, 0, q)
                each_expert(pool, body)

            @block.vector
            def _(v):
                def body(x, par, nxt):
                    with v.Fori(0, NQ) as q:
                        n = x * NQ + q
                        for c in range(3):
                            m = rows(c)
                            v.wait_ge(s_silu, n * 3 + c + 1)
                            v.wait_ge(s_dn, 1 + n * NT)
                            v.tensor_tensor(a[0:m, c, :], UP[c][0:m, :], silu[0:m, :], ALU.mult).then_inc(s_a, 1)
                            v.wait_ge(s_ah, 1 + n * 3 + c + 1)
                            v.tensor_tensor(al[0:m, c, :], a[0:m, c, :], ah[0:m, c, :].bitcast(F32), ALU.subtract).then_inc(s_al, 1)
                        for t in range(NT):
                            v.wait_ge(s_dn, 1 + n * NT + t + 1)
                            tile = bass.ds(q * NT + t, 1)
                            dst = acc[:, tile, :].rearrange("p a h -> p (a h)")
                            v.scalar_tensor_tensor(dst, DOWN[t % 2][:, :], comb[:, tile, bass.ds(x, 1)].rearrange("p a e -> p (a e)"),
                                                   dst, ALU.mult, ALU.add).then_inc(s_acc, 1)

                for q in range(NQ):
                    v.wait_ge(s_xh, q + 1)
                    tok = slice(q * S, (q + 1) * S)
                    v.tensor_tensor(xTl[:, :, tok], xTl[:, :, tok].bitcast(F32), xTh[:, :, tok].bitcast(F32),
                                    ALU.subtract).then_inc(s_xl, 1)
                each_expert(v, body)

            @block.tensor
            def _(pe):
                def body(x, par, nxt):
                    with pe.Fori(0, NQ) as q:
                        pe.wait_ge(s_lo, 1 + x * NQ + NQ)
                        n = x * NQ + q
                        tok = bass.ds(q * S, S)
                        for c, (o, m) in enumerate(CH):
                            pe.wait_ge(s_a, 1 + n * 3)
                            for dst, off in ((GATE[c], 0), (UP[c], I)):
                                i = 0
                                for wp, xp in ((w1h, xTh), (w1h, xTl), (w1l, xTh)):
                                    for k in range(NK):
                                        ins = pe.matmul(dst[0:m, :], wp[par][:, k, off + o:off + o + m], xp[:, k, tok],
                                                        start=(i == 0), stop=(i == 3 * NK - 1))
                                        i += 1
                            ins.then_inc(s_up, 1)

                        def down(t, c):
                            m = rows(c)
                            for j, (ap, wp) in enumerate(((ah, w2h), (ah, w2l), (al, w2h))):
                                ins = pe.matmul(DOWN[t % 2][:, :], ap[0:m, c, t * P:(t + 1) * P], wp[par][0:m, c, :],
                                                start=(c == 0 and j == 0), stop=(c == 2 and j == 2))
                            if c == 2:
                                ins.then_inc(s_dn, 1)

                        pe.wait_ge(s_al, n * 3 + 2)
                        for t in range(2):
                            pe.wait_ge(s_acc, 1 + n * NT)
                            down(t, 0)
                            down(t, 1)
                        pe.wait_ge(s_al, n * 3 + 3)
                        for t in range(2):
                            down(t, 2)
                        for t in range(2, NT):
                            pe.wait_ge(s_acc, 1 + n * NT + t - 1)
                            for c in range(3):
                                down(t, c)

                pe.wait_ge(s_xl, NQ)
                each_expert(pe, body)


def kernel(**inputs):
    import numpy as np
    import concourse.bacc as bacc
    from concourse import mybir as mb
    from concourse.bass_utils import run_bass_kernel_spmd

    def rope():
        inv = 1.0 / 10000.0 ** (np.arange(0, HD, 2, dtype=np.float32) / HD)
        freqs = np.einsum("i,j->ij", np.arange(S, dtype=np.float32), inv)
        emb = np.concatenate((freqs, freqs), axis=-1)
        rot = np.zeros((P, P), np.float32)
        for h in range(HG):
            for d in range(HD // 2):
                rot[h * HD + HD // 2 + d, h * HD + d] = -1.0
                rot[h * HD + d, h * HD + HD // 2 + d] = 1.0
        return np.tile(np.cos(emb).T, (HG, 1)), np.tile(np.sin(emb).T, (HG, 1)), rot

    cos, sin, rot = rope()
    mask = np.where(np.arange(P)[None, :] > np.arange(P)[:, None], np.float32(-1e30), np.float32(0))
    cst = np.concatenate([np.eye(P, dtype=np.float32), rot, mask, cos, sin], axis=1).astype(np.float32)

    g = {k: np.asarray(v) for k, v in inputs.items()}
    par = np.concatenate([g["L0_xattn_conv_w"], g["L0_xattn_conv_b"][:, None], g["L0_xattn_dt_proj_b"][:, None],
                          g["L0_xattn_D"][:, None], g["L0_xattn_A_log"]], axis=1)

    def chunks(w):
        return w.reshape(w.shape[0] // P, P, w.shape[1]).transpose(1, 0, 2)

    qkv = np.stack([chunks(g["L0_attn_W" + c].T) for c in "qkv"], axis=1)
    qkv = qkv.reshape(P, 3, NK, NG, P).transpose(3, 0, 1, 2, 4)
    sw1 = g["L0_ffn_shared_w1"].reshape(2, 2, I, H).transpose(1, 0, 2, 3).reshape(2, 2 * I, H)
    w1 = np.concatenate([g["L0_ffn_w1"], sw1]).transpose(0, 2, 1).reshape(NX, NK, P, 2 * I).transpose(0, 2, 1, 3)
    sw2 = g["L0_ffn_shared_w2"].T.reshape(2, I, H)
    w2 = np.concatenate([g["L0_ffn_w2"].transpose(0, 2, 1), sw2])
    arrays = {
        "x": g["x"].reshape(NB, NT, P, H).transpose(0, 2, 1, 3),
        "ctx": g["ctx_1024"].transpose(0, 2, 1).reshape(NB, 2, P, S).transpose(0, 2, 1, 3),
        "cst": cst,
        "par": par.reshape(NE, P, PAR).transpose(1, 0, 2),
        "wqkv": qkv,
        "wo": chunks(g["L0_attn_Wo"].T),
        "inw": chunks(g["L0_xattn_in_proj_w"].T),
        "xpw": chunks(g["L0_xattn_x_proj_w"].T),
        "dtw": g["L0_xattn_dt_proj_w"].T,
        "gate": chunks(g["L0_ffn_gate_w"].T),
        "w1": w1,
        "w2": w2,
    }
    arrays = {f"in_{k}": np.ascontiguousarray(v) for k, v in arrays.items()}
    nc = bacc.Bacc("TRN2", target_bir_lowering=False, num_devices=1)
    aps = {k: nc.dram_tensor(k, v.shape, mb.dt.from_np(v.dtype), kind="ExternalInput").ap() for k, v in arrays.items()}
    bc = nc.dram_tensor("bc_scratch", (NB, 2 * DS, S), mb.dt.float32, kind="Internal").ap()
    xt = nc.dram_tensor("xt_scratch", (NB, P, NK, S), mb.dt.float32, kind="Internal").ap()
    out = nc.dram_tensor("out_0", (P, NB * NT, H), mb.dt.float32, kind="ExternalOutput").ap()
    build(nc, *[aps["in_" + k] for k in ("x", "ctx", "cst", "par", "wqkv", "wo", "inw", "xpw", "dtw", "gate", "w1", "w2")],
          bc, xt, out)
    r = run_bass_kernel_spmd(nc, [arrays], core_ids=[0])
    return r.results[0]["out_0"].transpose(1, 0, 2).reshape(NB, S, H)
```

```python
from contextlib import ExitStack

import concourse.bass as bass
from concourse import mybir

F32 = mybir.dt.float32
F32R = mybir.dt.float32r
BF16 = mybir.dt.bfloat16
ALU = mybir.AluOpType
ACT = mybir.ActivationFunctionType
AX = mybir.AxisListType

P = 128
NB, S, H = 4, 512, 512
NT = S // P
NK = H // P
NH, HD = 16, 32
HG = P // HD
NG = NH // HG
SCALE = HD ** -0.5
EPS = 1e-5
DM, DI, DS, DC, DR = 256, 512, 16, 4, 16
NE = DI // P
NSG = DS // NG
STEPS = HG * NT
E, I, TOPK = 16, 352, 6
NX = E + 2
CH = [(0, 128), (128, 128), (256, 96)]
CST = 3 * P + 2 * S
PAR = 4 + 3 + DS


def build(nc, x_d, ctx_d, cst_d, par_d, wqkv_d, wo_d, inw_d, xpw_d, dtw_d, gate_d, w1_d, w2_d, bc_d, x2_d, xt_d, out_d):
    sems = ExitStack()

    def sem(name):
        return sems.enter_context(nc.semaphore(name))

    with sems, ExitStack() as whole:
        def keep(name, shape, dt=F32):
            return whole.enter_context(nc.sbuf_tensor(name, shape, dt))

        comb = keep("comb", [P, NB * NT, NX])
        bank = [whole.enter_context(nc.psum_tensor(f"bank{i}", [P, 512], F32)) for i in range(8)]

        mixer_phase(nc, sem, bank, comb, x_d, ctx_d, cst_d, par_d, wqkv_d, wo_d, inw_d, xpw_d,
                    dtw_d, gate_d, bc_d, x2_d, xt_d)
        expert_phase(nc, sem, bank, comb, x2_d, xt_d, w1_d, w2_d, out_d)


def mixer_phase(nc, sem, bank, comb, x_d, ctx_d, cst_d, par_d, wqkv_d, wo_d, inw_d, xpw_d,
                dtw_d, gate_d, bc_d, x2_d, xt_d):
    with ExitStack() as st:
        def sb(name, shape, dt=F32):
            return st.enter_context(nc.sbuf_tensor(name, shape, dt))

        cst = sb("cst", [P, CST])
        ident, rot, mask = cst[:, 0:P], cst[:, P:2 * P], cst[:, 2 * P:3 * P]
        cos, sin = cst[:, 3 * P:3 * P + S], cst[:, 3 * P + S:CST]
        identb = sb("identb", [P, P], BF16)
        maskb = sb("maskb", [P, P], BF16)
        par = sb("par", [P, NE, PAR])
        conv_w = lambda e, k: par[:, e, k:k + 1]
        conv_b = lambda e: par[:, e, 4:5]
        dt_b = lambda e: par[:, e, 5:6]
        aneg = sb("aneg", [P, NE, DS])
        aexp = sb("aexp", [P, NE, DS])
        diagD = sb("diagD", [P, NE, P])
        wo = sb("wo", [P, NG, H])
        inw = sb("inw", [P, 2, DI])
        xpw = sb("xpw", [P, NE, DR + 2 * DS])
        dtw = sb("dtw", [DR, DI])
        gw = sb("gw", [P, NK, E])
        eps = sb("eps", [P, 1])

        xin0 = sb("xin0", [P, NT, H])
        xb = sb("xb", [P, NT, H])
        ctxT = sb("ctxT", [P, 2, S])
        ln = sb("ln", [P, NT, H])
        lnT = sb("lnT", [P, NK, S])
        nothing = sb("nothing", [P, 1])
        stats = sb("stats", [P, NT, 6])
        mv = sb("mv", [P, NT, 2])
        lnv = sb("lnv", [P, NT])
        r0 = sb("r0", [P, NT])
        nt1 = sb("nt1", [P, NT])
        nt2 = sb("nt2", [P, NT])
        nt3 = sb("nt3", [P, NT])
        rstd = sb("rstd", [P, NT])
        xin = sb("xin", [P, NE, S + DC - 1])
        u = sb("u", [P, NE, S])
        delta = sb("delta", [P, NE, S])
        du = sb("du", [P, NE, S])
        xdbl = sb("xdbl", [DR + 2 * DS, S])
        bcn = sb("bcn", [P, 2, 2, S])
        dA = sb("dA", [P, 2, S])
        dBu = sb("dBu", [P, 2, S])
        hst = sb("hst", [P, 2, S])
        hC = sb("hC", [P, 2, S])

        wqkv = sb("wqkv", [P, NG, 3, NK, P])
        qraw = sb("qraw", [P, 2, S])
        qcos = sb("qcos", [P, 2, S])
        qsin = sb("qsin", [P, 2, S])
        qkall = sb("qkall", [P, NG, 2, S])
        vall = sb("vall", [P, NG, NT, P])
        qk = sb("qk", [P, 2, S])
        vg = sb("vg", [P, NT, P])
        prob = sb("prob", [P, 2, S])
        probT = sb("probT", [P, 2, S])
        mx = sb("mx", [P, STEPS])
        nmx = sb("nmx", [P, STEPS])
        rsum = sb("rsum", [P, STEPS])
        rinv = sb("rinv", [P, NG, STEPS])
        rrep = ln[:, :, :].rearrange("p g (t j d) -> p g t j d", t=NT, j=HG)
        ao = sb("ao", [P, NG, S])

        gmx = sb("gmx", [P, NT])
        gexp = sb("gexp", [P, NT, E])
        gsum = sb("gsum", [P, NT])
        grec = sb("grec", [P, NT])
        prb = sb("prb", [P, NT, E + 2])
        top8 = sb("top8", [P, NT, 8])
        rest = sb("rest", [P, NT, E + 2])

        Y = bank[0:4]
        S0, S1, TB, OB = bank[4:8]
        F4 = [S0, S1, TB, OB]

        s_const = sem("s_const")
        s_load = sem("s_load")
        s_wqkv = sem("s_wqkv")
        s_bcst = sem("s_bcst")
        s_bc = [sem(f"s_bc{i}") for i in range(2)]
        s_setup_a = sem("s_setup_a")
        s_setup_p = sem("s_setup_p")
        s_setup_v = sem("s_setup_v")
        s_var = sem("s_var")
        s_lnv = sem("s_lnv")
        s_r0 = sem("s_r0")
        s_ln = sem("s_ln")
        s_lnTp = sem("s_lnTp")
        s_lnT = sem("s_lnT")
        s_xinp = sem("s_xinp")
        s_xin = sem("s_xin")
        s_conv = sem("s_conv")
        s_tanh = sem("s_tanh")
        s_u = sem("s_u")
        s_xdp = sem("s_xdp")
        s_xd = sem("s_xd")
        s_dtp = sem("s_dtp")
        s_abs = sem("s_abs")
        s_relu = sem("s_relu")
        s_e = sem("s_e")
        s_l = sem("s_l")
        s_w1 = sem("s_w1")
        s_l2 = sem("s_l2")
        s_delta = sem("s_delta")
        s_du = sem("s_du")
        s_yinit = sem("s_yinit")
        s_qp = sem("s_qp")
        s_qraw = sem("s_qraw")
        s_v = sem("s_v")
        s_rotp = sem("s_rotp")
        s_qcos = sem("s_qcos")
        s_qsin = sem("s_qsin")
        s_qk = sem("s_qk")
        s_sc = sem("s_sc")
        s_mx = sem("s_mx")
        s_nmx = sem("s_nmx")
        s_prob = sem("s_prob")
        s_tp = sem("s_tp")
        s_pt = sem("s_pt")
        s_pv = sem("s_pv")
        s_dA = sem("s_dA")
        s_dBu = sem("s_dBu")
        s_scan = sem("s_scan")
        s_hC = sem("s_hC")
        s_y = sem("s_y")
        s_rinv = sem("s_rinv")
        s_rrep = sem("s_rrep")
        s_rbp = sem("s_rbp")
        s_ob = sem("s_ob")
        s_qks = sem("s_qks")
        s_vs = sem("s_vs")
        s_ao = sem("s_ao")
        s_wop = sem("s_wop")
        s_att = sem("s_att")
        s_th = sem("s_th")
        s_gz = sem("s_gz")
        s_yg = sem("s_yg")
        s_ytp = sem("s_ytp")
        s_x2 = sem("s_x2")
        s_xt = sem("s_xt")
        s_gp = sem("s_gp")
        s_gmx = sem("s_gmx")
        s_gexp = sem("s_gexp")
        s_gv = sem("s_gv")
        s_x2st = sem("s_x2st")
        s_small = sem("s_small")

        from_one = (s_att, s_qk, s_xt, s_x2st, s_bcst, s_tp, s_pv, s_y, s_gexp, s_yg, s_qcos, s_rotp, s_qraw, s_qsin, s_v, s_ao, s_ob,
                    s_sc)

        with nc.Block() as block:

            @block.sync
            def _(sp):
                for one in from_one:
                    sp.sem_inc(one, 1)
                for dst, src in ((cst[:, :], cst_d[:, :]), (par[:, :, :], par_d[:, :, :]), (inw[:, :, :], inw_d[:, :, :]),
                                 (xpw[:, :, :], xpw_d[:, :, :]), (dtw[:, :], dtw_d[:, :]), (gw[:, :, :], gate_d[:, :, :]),
                                 (wqkv[:, :, :, :, :], wqkv_d[:, :, :, :, :]), (wo[:, :, :], wo_d[:, :, :])):
                    sp.dma_start(dst, src).then_inc(s_const, 16)
                with sp.Fori(0, NB) as b:
                    sp.wait_ge(s_att, 1 + b * NT)
                    sp.dma_start(xin0[:, :, :], x_d[bass.ds(b, 1), :, :, :].rearrange("a p t h -> (a p) t h")).then_inc(s_load, 16)
                    sp.dma_start(ctxT[:, :, :], ctx_d[bass.ds(b, 1), :, :, :].rearrange("a p t h -> (a p) t h")).then_inc(s_load, 16)
                    sp.wait_ge(s_xd, b + 1)
                    sp.dma_start(bc_d[bass.ds(b, 1), :, :].rearrange("a r s -> (a r) s"), xdbl[DR:DR + 2 * DS, :]).then_inc(s_bcst, 16)
                    with sp.Fori(0, NG) as g:
                        it = b * NG + g
                        sp.wait_ge(s_bcst, 1 + b * 16 + 16)
                        for n in range(NSG):
                            sp.wait_ge(s_hC, (it * NSG + n) * NE + NE)
                            for row in range(2):
                                src = bc_d[bass.ds(b, 1), bass.ds(g * NSG + (row * DS + n), 1), :].rearrange("a r s -> (a r) s")
                                sp.dma_start(bcn[:, n % 2, row, :], src.to_broadcast([P, S])).then_inc(s_bc[n % 2], 16)
                sp.wait_ge(s_xt, 1 + NB * 16)
                sp.wait_ge(s_x2st, 1 + NB * 16)

            @block.gpsimd
            def _(pool):
                pool.memset(xin[:, :, 0:DC - 1], 0.0).then_inc(s_setup_p, 1)
                pool.memset(eps[:, :], EPS).then_inc(s_setup_p, 1)
                pool.memset(comb[:, :, E:NX], 1.0).then_inc(s_setup_p, 1)
                pool.memset(prb[:, :, E:E + 2], -1.0).then_inc(s_setup_p, 1)
                with pool.Fori(0, NB) as b:
                    for g in range(NG):
                        gi = b * NG + g
                        for c in range(2):
                            pool.wait_ge(s_qraw, 1 + gi * 2 + c + 1)
                            pool.wait_ge(s_qk, 1 + gi * 2)
                            pool.tensor_tensor(qcos[:, c, :], qraw[:, c, :], cos, ALU.mult).then_inc(s_qcos, 1)
                    for e in range(NE):
                        pool.wait_ge(s_w1, b * 2 * NE + NE + e + 1)
                        pool.wait_ge(s_l, b * NE + e + 1)
                        pool.tensor_tensor(ln[:, e, :], ln[:, e, :], xin[:, e, DC - 1:], ALU.subtract).then_inc(s_l2, 1)
                    for e in range(NE):
                        pool.wait_ge(s_l2, b * NE + e + 1)
                        pool.wait_ge(s_relu, b * NE + e + 1)
                        pool.tensor_tensor(delta[:, e, :], delta[:, e, :], ln[:, e, :], ALU.add).then_inc(s_delta, 1)
                    with pool.Fori(0, NG) as g:
                        it = b * NG + g
                        for s in range(STEPS):
                            n, e = divmod(s, NE)
                            if s == 0:
                                pool.wait_ge(s_du, b * NE + NE)
                            if e == 0:
                                pool.wait_ge(s_bc[n % 2], it * (NSG // 2) * 32 + (n // 2) * 32 + 32)
                            pool.wait_ge(s_scan, it * STEPS + s + 1)
                            pool.tensor_tensor(dBu[:, s % 2, :], du[:, e, :], bcn[:, n % 2, 0, :], ALU.mult).then_inc(s_dBu, 1)

            @block.scalar
            def _(act):
                act.wait_ge(s_const, 16 * 8)
                act.wait_ge(s_setup_p, 4)
                act.activation(aexp[:, :, :], par[:, :, 7:PAR], ACT.Exp).then_inc(s_setup_a, 1)
                act.activation(identb[:, :], ident, ACT.Copy).then_inc(s_setup_a, 1)
                act.activation(maskb[:, :], mask, ACT.Copy).then_inc(s_setup_a, 1)

                def rstd_guess(i):
                    act.wait_ge(s_var, i + 1)
                    act.activation(lnv[:, :], mv[:, :, 1], ACT.Ln, bias=eps[:, 0:1]).then_inc(s_lnv, 1)
                    act.wait_ge(s_lnv, i + 1)
                    act.activation(r0[:, :], lnv[:, :], ACT.Exp, scale=-0.5).then_inc(s_r0, 1)

                def copy_lnT(i):
                    for k in range(NK):
                        act.wait_ge(s_lnTp, i * NK + k + 1)
                        act.activation(lnT[:, k, :], F4[k][:, :], ACT.Copy).then_inc(s_lnT, 1)

                def copy_qkv(gi, g):
                    for c in range(2):
                        act.wait_ge(s_qp, gi * 3 + c + 1)
                        act.wait_ge(s_qcos, 1 + gi * 2)
                        act.wait_ge(s_rotp, 1 + gi * 2)
                        act.activation(qraw[:, c, :], Y[c][:, :], ACT.Copy).then_inc(s_qraw, 1)
                    act.wait_ge(s_qp, gi * 3 + 3)
                    act.activation(vall[:, g, :, :], Y[2][:, :].rearrange("p (t o) -> p t o", t=NT), ACT.Copy).then_inc(s_v, 1)

                act.preload_act_table_set("natural_log_exp_and_others")
                with act.Fori(0, NB) as b:
                    rstd_guess(b * 3)
                    for e in range(NE):
                        act.wait_ge(s_xinp, b * NE + e + 1)
                        act.activation(xin[:, e, DC - 1:], F4[e][:, :], ACT.Copy).then_inc(s_xin, 1)
                    act.wait_ge(s_xt, 1 + b * 16)
                    copy_lnT(b * 2)
                    copy_qkv(b * NG, 0)
                    for e in range(NE):
                        act.wait_ge(s_conv, b * NE * DC + NE * (DC - 1) + e + 1)
                        act.activation(delta[:, e, :], du[:, e, :], ACT.Tanh, scale=0.5).then_inc(s_tanh, 1)
                    copy_qkv(b * NG + 1, 1)
                    act.wait_ge(s_xdp, b + 1)
                    act.wait_ge(s_bcst, 1 + b * 16)
                    act.activation(xdbl[:, :], S0[0:DR + 2 * DS, :], ACT.Copy).then_inc(s_xd, 1)
                    copy_qkv(b * NG + 2, 2)
                    act.preload_act_table_set("natural_log_exp_and_others")
                    for e in range(NE):
                        act.wait_ge(s_dtp, b * NE + e + 1)
                        act.activation(ln[:, e, :], F4[e][:, :], ACT.Abs, bias=dt_b(e)).then_inc(s_abs, 1)
                    for e in range(NE):
                        act.wait_ge(s_abs, b * NE + e + 1)
                        act.activation(du[:, e, :], ln[:, e, :], ACT.Exp, scale=-1.0).then_inc(s_e, 1)
                    for e in range(NE):
                        act.wait_ge(s_e, b * NE + e + 1)
                        act.activation(ln[:, e, :], du[:, e, :], ACT.Ln, bias=1.0).then_inc(s_l, 1)
                    copy_qkv(b * NG + 3, 3)

                    with act.Fori(0, NG) as g:
                        it = b * NG + g
                        act.wait_ge(s_pv, 1 + it * STEPS)
                        act.wait_ge(s_v, 1 + b * NG + NG)
                        act.activation(vg[:, :, :], vall[:, bass.ds(g, 1), :, :].rearrange("p a t o -> p (a t) o"), ACT.Copy).then_inc(s_vs, 1)

                        def decay(s):
                            n, e = divmod(s, NE)
                            if s == 0:
                                act.wait_ge(s_delta, b * NE + NE)
                            act.wait_ge(s_scan, it * STEPS + s + 1)
                            act.activation(dA[:, s % 2, :], delta[:, e, :], ACT.Exp,
                                           scale=aneg[:, e, bass.ds(g * NSG + n, 1)]).then_inc(s_dA, 1)

                        def softmax(s):
                            w = (s % NT + 1) * P
                            act.wait_ge(s_nmx, it * STEPS + s + 1)
                            act.wait_ge(s_tp, 1 + it * STEPS + max(s - 1, 0))
                            act.activation(prob[:, s % 2, 0:w], [S0, S1][s % 2][:, 0:w], ACT.Exp, bias=nmx[:, s:s + 1],
                                           scale=SCALE, accum_out=rsum[:, s:s + 1]).then_inc(s_prob, 1)

                        def copy_probT(s):
                            w = (s % NT + 1) * P
                            act.wait_ge(s_tp, 1 + it * STEPS + s + 1)
                            act.wait_ge(s_pv, 1 + it * STEPS + max(s - 1, 0))
                            act.activation(probT[:, s % 2, 0:w], TB[:, 0:w], ACT.Copy).then_inc(s_pt, 1)

                        decay(0)
                        for k in range(STEPS + 1):
                            if k + 1 < STEPS:
                                decay(k + 1)
                            if k < STEPS:
                                softmax(k)
                            if k >= 1:
                                copy_probT(k - 1)
                        act.wait_ge(s_pv, 1 + it * STEPS + STEPS)
                        act.activation(ao[:, bass.ds(g, 1), :].rearrange("p a s -> p (a s)"), OB[:, :], ACT.Copy).then_inc(s_ob, 1)

                    rstd_guess(b * 3 + 1)
                    for t in range(NT):
                        act.wait_ge(s_ln, b * 3 * NT + NT + t + 1)
                        act.activation(delta[:, t, :], ln[:, t, :], ACT.Tanh, scale=0.5).then_inc(s_th, 1)
                    act.preload_act_table_set("natural_log_exp_and_others")
                    rstd_guess(b * 3 + 2)
                    copy_lnT(b * 2 + 1)
                    for t in range(NT):
                        act.wait_ge(s_gmx, b + 1)
                        act.activation(gexp[:, t, :], OB[:, t * E:(t + 1) * E], ACT.Exp, bias=gmx[:, t:t + 1],
                                       accum_out=gsum[:, t:t + 1]).then_inc(s_gexp, 1)
                    act.wait_ge(s_lnT, b * 2 * NK + 2 * NK)
                    act.dma_start(xt_d[bass.ds(b, 1), :, :, :].rearrange("a p k s -> (a p) k s"), lnT[:, :, :]).then_inc(s_xt, 16)
                    act.dma_start(x2_d[bass.ds(b, 1), :, :, :].rearrange("a p t h -> (a p) t h"), xb[:, :, :]).then_inc(s_x2st, 16)

            @block.vector
            def _(v):
                v.wait_ge(s_const, 16 * 8)
                v.wait_ge(s_setup_a, 3)
                v.tensor_scalar(aneg[:, :, :], aexp[:, :, :], -1.0, None, ALU.mult).then_inc(s_setup_v, 1)
                for e in range(NE):
                    v.tensor_scalar(diagD[:, e, :], ident, par[:, e, 6:7], None, ALU.mult).then_inc(s_setup_v, 1)
                v.sem_inc(s_scan, 2)
                v.sem_inc(s_hC, 2 * NE)

                class Chain:
                    n = 0
                    base = 0

                def link(ins, own_wait=False):
                    Chain.n += 1
                    ins.then_inc(s_small, 1)
                    v.wait_ge(s_small, Chain.base + Chain.n)
                    if own_wait:
                        v.memset(nothing[:, :], 0.0)

                def layer_norm(i, src):
                    for t in range(NT):
                        ins = v.bn_stats(stats[:, t, :], src[:, t, :])
                    link(ins, own_wait=True)
                    for t in range(NT):
                        ins = v.bn_aggr(mv[:, t, :], stats[:, t, :])
                    ins.then_inc(s_var, 1)
                    v.wait_ge(s_r0, i + 1)
                    link(v.tensor_tensor(nt1[:, :], r0[:, :], r0[:, :], ALU.mult))
                    link(v.scalar_tensor_tensor(nt2[:, :], mv[:, :, 1], EPS, nt1[:, :], ALU.add, ALU.mult))
                    link(v.tensor_scalar(nt3[:, :], nt2[:, :], -0.5, 1.5, ALU.mult, ALU.add))
                    link(v.tensor_tensor(rstd[:, :], r0[:, :], nt3[:, :], ALU.mult))
                    for t in range(NT):
                        v.tensor_scalar(ln[:, t, :], src[:, t, :], mv[:, t, 0:1], rstd[:, t:t + 1], ALU.subtract,
                                        ALU.mult).then_inc(s_ln, 1)

                def rotate(gi, g):
                    v.wait_ge(s_qk, 1 + gi * 2)
                    for c, src in ((0, Y[3]), (1, Y[1])):
                        v.wait_ge(s_rotp, 1 + gi * 2 + c + 1)
                        v.tensor_tensor(qsin[:, c, :], src[:, :], sin, ALU.mult).then_inc(s_qsin, 1)
                    for c in range(2):
                        v.wait_ge(s_qsin, 1 + gi * 2 + c + 1)
                        v.wait_ge(s_qcos, 1 + gi * 2 + c + 1)
                        v.tensor_tensor(qkall[:, g, c, :], qcos[:, c, :], qsin[:, c, :], ALU.add).then_inc(s_qk, 1)

                LINKS = 3 * 5 + 2 + 3 * NT
                with v.Fori(0, NB) as b:
                    Chain.n, Chain.base = 0, b * LINKS
                    v.wait_ge(s_load, b * 32 + 32)
                    layer_norm(b * 3, xin0)
                    for k in range(DC):
                        for e in range(NE):
                            n = b * NE * DC + NE * k + e
                            if k == 0:
                                v.wait_ge(s_xin, b * NE + e + 1)
                                v.tensor_scalar(du[:, e, :], xin[:, e, 0:S], conv_w(e, 0), conv_b(e), ALU.mult,
                                                ALU.add).then_inc(s_conv, 1)
                            else:
                                v.wait_ge(s_conv, n - NE + 1)
                                v.scalar_tensor_tensor(du[:, e, :], xin[:, e, k:k + S], conv_w(e, k), du[:, e, :],
                                                       ALU.mult, ALU.add).then_inc(s_conv, 1)
                    rotate(b * NG, 0)
                    for e in range(NE):
                        v.wait_ge(s_tanh, b * NE + e + 1)
                        v.scalar_tensor_tensor(u[:, e, :], delta[:, e, :], 1.0, du[:, e, :], ALU.add,
                                               ALU.mult).then_inc(s_u, 1)
                    for e in range(NE):
                        v.wait_ge(s_u, b * 2 * NE + e + 1)
                        v.tensor_scalar(u[:, e, :], u[:, e, :], 0.5, None, ALU.mult).then_inc(s_u, 1)
                    rotate(b * NG + 1, 1)
                    rotate(b * NG + 2, 2)
                    for e in range(NE):
                        v.wait_ge(s_abs, b * NE + NE)
                        v.tensor_scalar(delta[:, e, :], F4[e][:, :], dt_b(e), 0.0, ALU.add, ALU.max).then_inc(s_relu, 1)
                    for e in range(NE):
                        v.wait_ge(s_e, b * NE + e + 1)
                        v.tensor_scalar(xin[:, e, DC - 1:], du[:, e, :], 1.0, 1.0, ALU.add, ALU.subtract).then_inc(s_w1, 1)
                    for e in range(NE):
                        v.wait_ge(s_w1, b * 2 * NE + e + 1)
                        v.tensor_tensor(xin[:, e, DC - 1:], xin[:, e, DC - 1:], du[:, e, :], ALU.subtract).then_inc(s_w1, 1)

                    for e in range(NE):
                        v.wait_ge(s_l2, b * NE + e + 1)
                        v.wait_ge(s_delta, b * NE + e + 1)
                        v.tensor_tensor(du[:, e, :], delta[:, e, :], u[:, e, :], ALU.mult).then_inc(s_du, 1)
                    rotate(b * NG + 3, 3)

                    with v.Fori(0, NG) as g:
                        it = b * NG + g
                        v.wait_ge(s_qk, 1 + b * 2 * NG + 2 * NG)
                        v.wait_ge(s_sc, 1 + it * STEPS)
                        v.tensor_copy(qk[:, :, :], qkall[:, bass.ds(g, 1), :, :].rearrange("p a c s -> p (a c) s")).then_inc(s_qks, 1)

                        def c_product(s):
                            n = s // NE
                            v.wait_ge(s_scan, it * STEPS + s + 3)
                            v.wait_ge(s_y, 1 + it * STEPS + max(s - 1, 0))
                            v.tensor_tensor(hC[:, s % 2, :], hst[:, s % 2, :], bcn[:, n % 2, 1, :], ALU.mult).then_inc(s_hC, 1)

                        for s in range(STEPS):
                            w = (s % NT + 1) * P
                            v.wait_ge(s_sc, 1 + it * STEPS + s + 1)
                            v.tensor_reduce(mx[:, s:s + 1], [S0, S1][s % 2][:, 0:w], AX.X, ALU.max).then_inc(s_mx, 1)
                            v.wait_ge(s_dA, it * STEPS + s + 1)
                            v.wait_ge(s_dBu, it * STEPS + s + 1)
                            v.wait_ge(s_hC, it * STEPS + s - 1 + 2 * NE)
                            v.tensor_tensor_scan(hst[:, s % 2, :], dA[:, s % 2, :], dBu[:, s % 2, :], 0.0, ALU.mult,
                                                 ALU.add).then_inc(s_scan, 1)
                            v.wait_ge(s_mx, it * STEPS + s + 1)
                            v.tensor_scalar(nmx[:, s:s + 1], mx[:, s:s + 1], -SCALE, None, ALU.mult).then_inc(s_nmx, 1)
                            if s >= 1:
                                c_product(s - 1)
                        c_product(STEPS - 1)

                        v.wait_ge(s_prob, it * STEPS + STEPS)
                        v.reciprocal(rinv[:, bass.ds(g, 1), :].rearrange("p a s -> p (a s)"), rsum[:, :]).then_inc(s_rinv, 1)

                    for g in range(NG):
                        v.wait_ge(s_rinv, b * NG + NG)
                        v.tensor_copy(rrep[:, g, :, :, :],
                                      rinv[:, g, :].rearrange("p (j t) -> p t j", t=NT).unsqueeze(3).to_broadcast([P, NT, HG, HD])
                                      ).then_inc(s_rrep, 1)
                    for g in range(NG):
                        v.wait_ge(s_rbp, b * NG + g + 1)
                        v.wait_ge(s_ob, 1 + b * NG + NG)
                        v.tensor_tensor(ao[:, g, :], F4[g][:, :], ao[:, g, :], ALU.mult).then_inc(s_ao, 1)
                    for t in range(NT):
                        v.wait_ge(s_wop, b * NT + t + 1)
                        v.wait_ge(s_x2st, 1 + b * 16)
                        v.tensor_tensor(xb[:, t, :], F4[t][:, :], xin0[:, t, :], ALU.add).then_inc(s_att, 1)
                    v.wait_ge(s_att, 1 + b * NT + NT)
                    layer_norm(b * 3 + 1, xb)
                    for t in range(NT):
                        v.wait_ge(s_th, b * NT + t + 1)
                        v.scalar_tensor_tensor(ln[:, t, :], delta[:, t, :], 1.0, ln[:, t, :], ALU.add,
                                               ALU.mult).then_inc(s_gz, 1)
                    for t in range(NT):
                        v.wait_ge(s_gz, b * NT + t + 1)
                        v.wait_ge(s_y, 1 + (b * NG + NG) * STEPS)
                        v.scalar_tensor_tensor(u[:, t, :], ln[:, t, :], 0.5, Y[t][:, :], ALU.mult,
                                               ALU.mult).then_inc(s_yg, 1)
                    for t in range(NT):
                        v.wait_ge(s_ytp, b * NT + t + 1)
                        v.tensor_tensor(xb[:, t, :], F4[t][:, :], xb[:, t, :], ALU.add).then_inc(s_x2, 1)
                    v.wait_ge(s_x2, b * NT + NT)
                    layer_norm(b * 3 + 2, xb)
                    v.wait_ge(s_gp, b * NT + NT)
                    v.tensor_reduce(gmx[:, :], OB[:, 0:NT * E].rearrange("p (t e) -> p t e", t=NT), AX.X, ALU.max,
                                    negate=True).then_inc(s_gmx, 1)
                    v.wait_ge(s_gexp, 1 + b * NT + NT)
                    link(v.reciprocal(grec[:, :], gsum[:, :]))
                    for t in range(NT):
                        ins = v.tensor_scalar(prb[:, t, 0:E], gexp[:, t, :], grec[:, t:t + 1], None, ALU.mult)
                    link(ins, own_wait=True)
                    for t in range(NT):
                        link(v.max(top8[:, t, :], prb[:, t, 0:E]))
                        link(v.memset(top8[:, t, TOPK:8], -1.0), own_wait=True)
                        link(v.match_replace(rest[:, t, :], top8[:, t, :], prb[:, t, :], 0.0))
                        v.tensor_tensor(comb[:, bass.ds(b * NT + t, 1), 0:E].rearrange("p a e -> p (a e)"), prb[:, t, 0:E],
                                        rest[:, t, 0:E], ALU.subtract).then_inc(s_gv, 1)
                    assert Chain.n == LINKS, Chain.n

            @block.tensor
            def _(pe):
                pe.wait_ge(s_const, 16 * 8)
                pe.wait_ge(s_setup_v, 1 + NE)

                def transpose_ln(b, which):
                    for k in range(NK):
                        for t in range(NT):
                            if k == 0:
                                pe.wait_ge(s_ln, b * 3 * NT + which * NT + t + 1)
                            ins = pe.transpose(F4[k][:, t * P:(t + 1) * P], ln[:, t, k * P:(k + 1) * P], ident)
                        ins.then_inc(s_lnTp, 1)

                def project_qkv(gi, g):
                    pe.wait_ge(s_qraw, 1 + gi * 2)
                    for k in range(NK):
                        ins = pe.matmul(Y[0][:, :], wqkv[:, g, 0, k, :], lnT[:, k, :], start=(k == 0), stop=(k == NK - 1))
                    ins.then_inc(s_qp, 1)
                    pe.wait_ge(s_qsin, 1 + gi * 2)
                    for k in range(NK):
                        ins = pe.matmul(Y[1][:, :], wqkv[:, g, 1, k, :], lnT[:, k, :], start=(k == 0), stop=(k == NK - 1))
                    ins.then_inc(s_qp, 1)
                    pe.wait_ge(s_qraw, 1 + gi * 2 + 1)
                    pe.matmul(Y[3][:, :], rot, qraw[:, 0, :], start=True, stop=True).then_inc(s_rotp, 1)
                    pe.wait_ge(s_v, 1 + gi)
                    for t in range(NT):
                        for k in range(NK):
                            ins = pe.matmul(Y[2][:, t * P:(t + 1) * P], lnT[:, k, t * P:(t + 1) * P], wqkv[:, g, 2, k, :],
                                            start=(k == 0), stop=(k == NK - 1))
                    ins.then_inc(s_qp, 1)
                    pe.wait_ge(s_qraw, 1 + gi * 2 + 2)
                    pe.matmul(Y[1][:, :], rot, qraw[:, 1, :], start=True, stop=True).then_inc(s_rotp, 1)

                with pe.Fori(0, NB) as b:
                    pe.wait_ge(s_gexp, 1 + b * NT)
                    pe.wait_ge(s_load, b * 32 + 32)
                    for e in range(NE):
                        for k in range(2):
                            ins = pe.matmul(F4[e][:, :], inw[:, k, e * P:(e + 1) * P], ctxT[:, k, :], start=(k == 0),
                                            stop=(k == 1))
                        ins.then_inc(s_xinp, 1)
                    pe.wait_ge(s_xin, b * NE + NE)
                    transpose_ln(b, 0)
                    pe.wait_ge(s_yg, 1 + b * NT)
                    pe.wait_ge(s_lnT, b * 2 * NK + NK)
                    project_qkv(b * NG, 0)
                    project_qkv(b * NG + 1, 1)
                    for e in range(NE):
                        pe.wait_ge(s_u, b * 2 * NE + NE + e + 1)
                        ins = pe.matmul(S0[0:DR + 2 * DS, :], xpw[:, e, :], u[:, e, :], start=(e == 0), stop=(e == NE - 1))
                    ins.then_inc(s_xdp, 1)
                    project_qkv(b * NG + 2, 2)
                    pe.wait_ge(s_xd, b + 1)
                    for e in range(NE):
                        pe.matmul(F4[e][:, :], dtw[:, e * P:(e + 1) * P], xdbl[0:DR, :], start=True, stop=True).then_inc(s_dtp, 1)
                    project_qkv(b * NG + 3, 3)
                    pe.wait_ge(s_qsin, 1 + b * 2 * NG + 2 * NG)
                    pe.wait_ge(s_v, 1 + b * NG + NG)
                    for e in range(NE):
                        ins = pe.matmul(Y[e][:, :], diagD[:, e, :], u[:, e, :], start=True, stop=False, skip_group_check=True)
                    ins.then_inc(s_yinit, 1)

                    with pe.Fori(0, NG) as g:
                        it = b * NG + g
                        pe.wait_ge(s_relu, b * NE + NE)

                        def scores(s):
                            j, t = divmod(s, NT)
                            r = slice(j * HD, (j + 1) * HD)
                            if s == 0:
                                pe.wait_ge(s_qks, it + 1)
                            if s >= 2:
                                pe.wait_ge(s_prob, it * STEPS + s - 1)
                            dst = [S0, S1][s % 2]
                            w = (t + 1) * P
                            pe.matmul(dst[:, 0:w], qk[r, 0, t * P:w], qk[r, 1, 0:w], start=True, stop=False)
                            pe.matmul(dst[:, t * P:w], identb[:, :], maskb[:, :], start=False, stop=True).then_inc(s_sc, 1)

                        def transposes(s):
                            t = s % NT
                            pe.wait_ge(s_prob, it * STEPS + s + 1)
                            if s == 0:
                                pe.wait_ge(s_vs, it + 1)
                            else:
                                pe.wait_ge(s_pt, it * STEPS + s)
                            for k in range(t + 1):
                                ins = pe.transpose(TB[:, k * P:(k + 1) * P], prob[:, s % 2, k * P:(k + 1) * P], ident)
                            ins.then_inc(s_tp, 1)

                        def values(s):
                            j, t = divmod(s, NT)
                            pe.wait_ge(s_pt, it * STEPS + s + 1)
                            if s == 0:
                                pe.wait_ge(s_ob, 1 + it)
                            for k in range(t + 1):
                                ins = pe.matmul(OB[j * HD:(j + 1) * HD, t * P:(t + 1) * P], vg[:, k, j * HD:(j + 1) * HD],
                                                probT[:, s % 2, k * P:(k + 1) * P], start=(k == 0), stop=(k == t))
                            ins.then_inc(s_pv, 1)

                        def sum_states(s):
                            e = s % NE
                            pe.wait_ge(s_hC, it * STEPS + s + 1 + 2 * NE)
                            pe.matmul(Y[e][:, :], ident, hC[:, s % 2, :], start=False, stop=False,
                                      skip_group_check=True).then_inc(s_y, 1)

                        scores(0)
                        for k in range(STEPS + 2):
                            if k + 1 < STEPS:
                                scores(k + 1)
                            if 1 <= k <= STEPS:
                                transposes(k - 1)
                            if k >= 2:
                                values(k - 2)
                                sum_states(k - 2)

                    pe.wait_ge(s_ob, 1 + b * NG + NG)
                    for g in range(NG):
                        pe.wait_ge(s_rrep, b * NG + g + 1)
                        for t in range(NT):
                            ins = pe.matmul(F4[g][:, t * P:(t + 1) * P], rrep[:, g, t, :, :].rearrange("p j d -> p (j d)"), ident,
                                            start=True, stop=True)
                        ins.then_inc(s_rbp, 1)
                    pe.wait_ge(s_ao, 1 + b * NG + NG)
                    for t in range(NT):
                        for g in range(NG):
                            ins = pe.matmul(F4[t][:, :], ao[:, g, t * P:(t + 1) * P], wo[:, g, :], start=(g == 0),
                                            stop=(g == NG - 1))
                        ins.then_inc(s_wop, 1)

                    pe.wait_ge(s_att, 1 + b * NT + NT)
                    for t in range(NT):
                        for e in range(NE):
                            pe.wait_ge(s_yg, 1 + b * NT + e + 1)
                            ins = pe.transpose(F4[t][:, e * P:(e + 1) * P], u[:, e, t * P:(t + 1) * P], ident)
                        ins.then_inc(s_ytp, 1)
                    pe.wait_ge(s_x2, b * NT + NT)
                    transpose_ln(b, 2)
                    pe.wait_ge(s_lnT, b * 2 * NK + 2 * NK)
                    for t in range(NT):
                        for k in range(NK):
                            ins = pe.matmul(OB[:, t * E:(t + 1) * E], lnT[:, k, t * P:(t + 1) * P], gw[:, k, :],
                                            start=(k == 0), stop=(k == NK - 1))
                        ins.then_inc(s_gp, 1)


def expert_phase(nc, sem, bank, comb, x2_d, xt_d, w1_d, w2_d, out_d):
    with ExitStack() as st:
        def sb(name, shape, dt=F32):
            return st.enter_context(nc.sbuf_tensor(name, shape, dt))

        xTh = sb("xTh", [P, NK, NB * S], F32R)
        xTl = sb("xTl", [P, NK, NB * S], F32R)
        acc = sb("acc", [P, NB * NT, H])
        NQ = NB
        raw1 = sb("raw1", [P, NK, 2 * I])
        raw2 = sb("raw2", [P, 3, H])
        w1h = [sb(f"w1h{i}", [P, NK, 2 * I], F32R) for i in range(2)]
        w1l = [sb(f"w1l{i}", [P, NK, 2 * I], F32R) for i in range(2)]
        w2h = [sb(f"w2h{i}", [P, 3, H], F32R) for i in range(2)]
        w2l = [sb(f"w2l{i}", [P, 3, H], F32R) for i in range(2)]
        silu = sb("silu", [P, S])
        a = sb("a", [P, 3, S])
        ah = sb("ah", [P, 3, S], F32R)
        al = sb("al", [P, 3, S], F32R)
        GATE, UP = [bank[0], bank[2], bank[4]], [bank[1], bank[3], bank[5]]
        DOWN = bank[6:8]

        s_zero = sem("s_zero")
        s_x = sem("s_x")
        s_xh = sem("s_xh")
        s_xl = sem("s_xl")
        s_raw = sem("s_raw")
        s_hi = sem("s_whi")
        s_lo = sem("s_wlo")
        s_up = sem("s_up")
        s_silu = sem("s_silu")
        s_a = sem("s_a")
        s_ah = sem("s_ah")
        s_al = sem("s_al")
        s_dn = sem("s_dn")
        s_acc = sem("s_acc")
        s_out = sem("s_out")
        PAIRS = NX // 2

        def rows(c):
            return CH[c][1]

        def each_expert(eng, body):
            with eng.Fori(0, PAIRS - 1) as pr:
                body(pr * 2, 0, True)
                body(pr * 2 + 1, 1, True)
            body(NX - 2, 0, True)
            body(NX - 1, 1, False)

        from_one = (s_lo, s_hi, s_a, s_dn, s_ah, s_acc)

        with nc.Block() as block:

            @block.sync
            def _(sp):
                for one in from_one:
                    sp.sem_inc(one, 1)
                for q in range(NQ):
                    sp.dma_start(xTl[:, :, q * S:(q + 1) * S].bitcast(F32), xt_d[q]).then_inc(s_x, 16)
                    sp.dma_start(acc[:, q * NT:(q + 1) * NT, :], x2_d[q]).then_inc(s_x, 16)
                sp.wait_ge(s_zero, 1)
                with sp.Fori(0, NX) as x:
                    sp.wait_ge(s_lo, 1 + x * NQ)
                    sp.wait_ge(s_hi, 1 + x * NQ)
                    sp.dma_start(raw1[:, :, :], w1_d[bass.ds(x, 1), :, :, :].rearrange("a p k o -> (a p) k o")).then_inc(s_raw, 16)
                    w2x = w2_d[bass.ds(x, 1), :, :].rearrange("a i h -> (a i) h")
                    sp.dma_start(raw2[:, 0:2, :], w2x[0:2 * P, :].rearrange("(c p) h -> p c h", p=P)).then_inc(s_raw, 16)
                    sp.dma_start(raw2[0:I - 2 * P, 2, :], w2x[2 * P:I, :]).then_inc(s_raw, 16)
                sp.wait_ge(s_acc, 1 + NX * NQ * NT)
                sp.dma_start(out_d[:, :, :], acc[:, :, :]).then_inc(s_out, 16)
                sp.wait_ge(s_out, 16)

            @block.scalar
            def _(act):
                def split_hi(x, par, q):
                    act.wait_ge(s_raw, x * 48 + 48)
                    act.activation(w1h[par][:, bass.ds(q, 1), :], raw1[:, bass.ds(q, 1), :], ACT.Copy)
                    act.activation(w2h[par][:, :, bass.ds(q * P, P)], raw2[:, :, bass.ds(q * P, P)], ACT.Copy).then_inc(s_hi, 1)

                def body(x, par, nxt):
                    with act.Fori(0, NQ) as q:
                        n = x * NQ + q
                        for c in range(3):
                            m = rows(c)
                            act.wait_ge(s_up, n * 3 + c + 1)
                            act.wait_ge(s_a, 1 + n * 3 + c)
                            act.activation(silu[0:m, :], GATE[c][0:m, :], ACT.Silu).then_inc(s_silu, 1)
                            if c == 0 and nxt:
                                act.wait_ge(s_dn, 1 + x * NQ * NT)
                                split_hi(x + 1, 1 - par, q)
                            act.wait_ge(s_a, 1 + n * 3 + c + 1)
                            act.wait_ge(s_dn, 1 + n * NT)
                            act.activation(ah[0:m, c, :], a[0:m, c, :], ACT.Copy).then_inc(s_ah, 1)

                with act.Fori(0, NQ) as q:
                    split_hi(0, 0, q)
                for q in range(NQ):
                    act.wait_ge(s_x, NQ * 32)
                    tok = slice(q * S, (q + 1) * S)
                    act.activation(xTh[:, :, tok], xTl[:, :, tok].bitcast(F32), ACT.Copy).then_inc(s_xh, 1)
                each_expert(act, body)

            @block.gpsimd
            def _(pool):
                pool.memset(raw2[:, 2, :], 0.0).then_inc(s_zero, 1)

                def split_lo(x, par, q):
                    pool.wait_ge(s_hi, 1 + x * NQ + q + 1)
                    sl = bass.ds(q * P, P)
                    pool.tensor_tensor(w1l[par][:, bass.ds(q, 1), :], raw1[:, bass.ds(q, 1), :],
                                       w1h[par][:, bass.ds(q, 1), :].bitcast(F32), ALU.subtract)
                    pool.tensor_tensor(w2l[par][:, :, sl], raw2[:, :, sl], w2h[par][:, :, sl].bitcast(F32),
                                       ALU.subtract).then_inc(s_lo, 1)

                def body(x, par, nxt):
                    if nxt:
                        with pool.Fori(0, NQ) as q:
                            split_lo(x + 1, 1 - par, q)

                with pool.Fori(0, NQ) as q:
                    split_lo(0, 0, q)
                each_expert(pool, body)

            @block.vector
            def _(v):
                def body(x, par, nxt):
                    with v.Fori(0, NQ) as q:
                        n = x * NQ + q
                        for c in range(3):
                            m = rows(c)
                            v.wait_ge(s_silu, n * 3 + c + 1)
                            v.wait_ge(s_dn, 1 + n * NT)
                            v.tensor_tensor(a[0:m, c, :], UP[c][0:m, :], silu[0:m, :], ALU.mult).then_inc(s_a, 1)
                            v.wait_ge(s_ah, 1 + n * 3 + c + 1)
                            v.tensor_tensor(al[0:m, c, :], a[0:m, c, :], ah[0:m, c, :].bitcast(F32), ALU.subtract).then_inc(s_al, 1)
                        for t in range(NT):
                            v.wait_ge(s_dn, 1 + n * NT + t + 1)
                            tile = bass.ds(q * NT + t, 1)
                            dst = acc[:, tile, :].rearrange("p a h -> p (a h)")
                            v.scalar_tensor_tensor(dst, DOWN[t % 2][:, :], comb[:, tile, bass.ds(x, 1)].rearrange("p a e -> p (a e)"),
                                                   dst, ALU.mult, ALU.add).then_inc(s_acc, 1)

                for q in range(NQ):
                    v.wait_ge(s_xh, q + 1)
                    tok = slice(q * S, (q + 1) * S)
                    v.tensor_tensor(xTl[:, :, tok], xTl[:, :, tok].bitcast(F32), xTh[:, :, tok].bitcast(F32),
                                    ALU.subtract).then_inc(s_xl, 1)
                each_expert(v, body)

            @block.tensor
            def _(pe):
                def body(x, par, nxt):
                    with pe.Fori(0, NQ) as q:
                        pe.wait_ge(s_lo, 1 + x * NQ + NQ)
                        n = x * NQ + q
                        tok = bass.ds(q * S, S)
                        for c, (o, m) in enumerate(CH):
                            pe.wait_ge(s_a, 1 + n * 3)
                            for dst, off in ((GATE[c], 0), (UP[c], I)):
                                i = 0
                                for wp, xp in ((w1h, xTh), (w1h, xTl), (w1l, xTh)):
                                    for k in range(NK):
                                        ins = pe.matmul(dst[0:m, :], wp[par][:, k, off + o:off + o + m], xp[:, k, tok],
                                                        start=(i == 0), stop=(i == 3 * NK - 1))
                                        i += 1
                            ins.then_inc(s_up, 1)

                        def down(t, c):
                            m = rows(c)
                            for j, (ap, wp) in enumerate(((ah, w2h), (ah, w2l), (al, w2h))):
                                ins = pe.matmul(DOWN[t % 2][:, :], ap[0:m, c, t * P:(t + 1) * P], wp[par][0:m, c, :],
                                                start=(c == 0 and j == 0), stop=(c == 2 and j == 2))
                            if c == 2:
                                ins.then_inc(s_dn, 1)

                        pe.wait_ge(s_al, n * 3 + 2)
                        for t in range(2):
                            pe.wait_ge(s_acc, 1 + n * NT)
                            down(t, 0)
                            down(t, 1)
                        pe.wait_ge(s_al, n * 3 + 3)
                        for t in range(2):
                            down(t, 2)
                        for t in range(2, NT):
                            pe.wait_ge(s_acc, 1 + n * NT + t - 1)
                            for c in range(3):
                                down(t, c)

                pe.wait_ge(s_xl, NQ)
                each_expert(pe, body)


def kernel(**inputs):
    import numpy as np
    import concourse.bacc as bacc
    from concourse import mybir as mb
    from concourse.bass_utils import run_bass_kernel_spmd

    def rope():
        inv = 1.0 / 10000.0 ** (np.arange(0, HD, 2, dtype=np.float32) / HD)
        freqs = np.einsum("i,j->ij", np.arange(S, dtype=np.float32), inv)
        emb = np.concatenate((freqs, freqs), axis=-1)
        rot = np.zeros((P, P), np.float32)
        for h in range(HG):
            for d in range(HD // 2):
                rot[h * HD + HD // 2 + d, h * HD + d] = -1.0
                rot[h * HD + d, h * HD + HD // 2 + d] = 1.0
        return np.tile(np.cos(emb).T, (HG, 1)), np.tile(np.sin(emb).T, (HG, 1)), rot

    cos, sin, rot = rope()
    mask = np.where(np.arange(P)[None, :] > np.arange(P)[:, None], np.float32(-1e30), np.float32(0))
    cst = np.concatenate([np.eye(P, dtype=np.float32), rot, mask, cos, sin], axis=1).astype(np.float32)

    g = {k: np.asarray(v) for k, v in inputs.items()}
    par = np.concatenate([g["L0_xattn_conv_w"], g["L0_xattn_conv_b"][:, None], g["L0_xattn_dt_proj_b"][:, None],
                          g["L0_xattn_D"][:, None], g["L0_xattn_A_log"]], axis=1)

    def chunks(w):
        return w.reshape(w.shape[0] // P, P, w.shape[1]).transpose(1, 0, 2)

    qkv = np.stack([chunks(g["L0_attn_W" + c].T) for c in "qkv"], axis=1)
    qkv = qkv.reshape(P, 3, NK, NG, P).transpose(0, 3, 1, 2, 4)
    sw1 = g["L0_ffn_shared_w1"].reshape(2, 2, I, H).transpose(1, 0, 2, 3).reshape(2, 2 * I, H)
    w1 = np.concatenate([g["L0_ffn_w1"], sw1]).transpose(0, 2, 1).reshape(NX, NK, P, 2 * I).transpose(0, 2, 1, 3)
    sw2 = g["L0_ffn_shared_w2"].T.reshape(2, I, H)
    w2 = np.concatenate([g["L0_ffn_w2"].transpose(0, 2, 1), sw2])
    arrays = {
        "x": g["x"].reshape(NB, NT, P, H).transpose(0, 2, 1, 3),
        "ctx": g["ctx_1024"].transpose(0, 2, 1).reshape(NB, 2, P, S).transpose(0, 2, 1, 3),
        "cst": cst,
        "par": par.reshape(NE, P, PAR).transpose(1, 0, 2),
        "wqkv": qkv,
        "wo": chunks(g["L0_attn_Wo"].T),
        "inw": chunks(g["L0_xattn_in_proj_w"].T),
        "xpw": chunks(g["L0_xattn_x_proj_w"].T),
        "dtw": g["L0_xattn_dt_proj_w"].T,
        "gate": chunks(g["L0_ffn_gate_w"].T),
        "w1": w1,
        "w2": w2,
    }
    arrays = {f"in_{k}": np.ascontiguousarray(v) for k, v in arrays.items()}
    nc = bacc.Bacc("TRN2", target_bir_lowering=False, num_devices=1)
    aps = {k: nc.dram_tensor(k, v.shape, mb.dt.from_np(v.dtype), kind="ExternalInput").ap() for k, v in arrays.items()}
    bc = nc.dram_tensor("bc_scratch", (NB, 2 * DS, S), mb.dt.float32, kind="Internal").ap()
    x2 = nc.dram_tensor("x2_scratch", (NB, P, NT, H), mb.dt.float32, kind="Internal").ap()
    xt = nc.dram_tensor("xt_scratch", (NB, P, NK, S), mb.dt.float32, kind="Internal").ap()
    out = nc.dram_tensor("out_0", (P, NB * NT, H), mb.dt.float32, kind="ExternalOutput").ap()
    build(nc, *[aps["in_" + k] for k in ("x", "ctx", "cst", "par", "wqkv", "wo", "inw", "xpw", "dtw", "gate", "w1", "w2")],
          bc, x2, xt, out)
    r = run_bass_kernel_spmd(nc, [arrays], core_ids=[0])
    return r.results[0]["out_0"].transpose(1, 0, 2).reshape(NB, S, H)
```

```python
from contextlib import ExitStack

import concourse.bass as bass
from concourse import mybir

F32 = mybir.dt.float32
F32R = mybir.dt.float32r
BF16 = mybir.dt.bfloat16
ALU = mybir.AluOpType
ACT = mybir.ActivationFunctionType
AX = mybir.AxisListType

P = 128
NB, S, H = 4, 512, 512
NT = S // P
NK = H // P
NH, HD = 16, 32
HG = P // HD
NG = NH // HG
SCALE = HD ** -0.5
EPS = 1e-5
DM, DI, DS, DC, DR = 256, 512, 16, 4, 16
NE = DI // P
NSG = DS // NG
STEPS = HG * NT
PAIRS = STEPS // 2
ADDED = [q for q in range(PAIRS) if q % NE != NE - 1]
SUMS = len(ADDED) + 2 * (PAIRS - len(ADDED))
RING = 6
E, I, TOPK = 16, 352, 6
SH = 2
NX = SH + E
BLK = 256
HALVES = BLK // P
TOK = NB * S
NBLK = TOK // BLK
NJ = TOK // P
ROWS = TOK + BLK
CH = [(0, 128), (128, 128), (256, 96)]
CST = 4 * P + 2 * S + E + 1
PAR = 4 + 3 + DS


def pairs_added(q):
    return sum(p <= q for p in ADDED)


def sums_made(s):
    return sum(1 if q in ADDED else min(s - 2 * q + 1, 2) for q in range(s // 2 + 1))


def scan_step(s):
    return s // (2 * NE) * 2 + s % 2, s % (2 * NE) // 2


def build(nc, x_d, ctx_d, cst_d, par_d, wqkv_d, wo_d, inw_d, xpw_d, dtw_d, gate_d, w1_d, w2_d, bc_d, slots0_d,
          slots_d, xn_d, out_d):
    sems = ExitStack()

    def sem(name):
        return sems.enter_context(nc.semaphore(name))

    with sems, ExitStack() as whole:
        def keep(name, shape, dt=F32):
            return whole.enter_context(nc.sbuf_tensor(name, shape, dt))

        cst = keep("cst", [P, CST])
        counts = keep("counts", [P, E])
        slot = keep("slot", [P, NT, TOPK], mybir.dt.uint32)
        entry = keep("entry", [P, NT, TOPK, 2], mybir.dt.int32)
        s_slot = sem("s_slot")
        s_slots = sem("s_slots")
        bank = [whole.enter_context(nc.psum_tensor(f"bank{i}", [P, 512], F32)) for i in range(8)]

        mixer_phase(nc, sem, bank, cst, x_d, ctx_d, cst_d, par_d, wqkv_d, wo_d, inw_d, xpw_d,
                    dtw_d, gate_d, bc_d, slots0_d, slots_d, xn_d, out_d, counts, slot, entry, s_slot, s_slots)
        expert_phase(nc, sem, bank, cst, counts, slot, entry, s_slot, s_slots, slots_d, xn_d, w1_d, w2_d, out_d)


def fill_slots(pool, b, first, last, slot, entry, s_slot, s_slots, s_carry, slots_d):
    if first == 0:
        pool.wait_ge(s_slots, 16 + b * NT * TOPK * 16)
        pool.sem_inc(s_carry, 1)
        pool.wait_ge(s_slot, b + 1)
        pool.sem_inc(s_carry, 1)
    for i in range(first, last):
        t, k = divmod(i, TOPK)
        pool.indirect_dma_start(out=slots_d[:, :], out_offset=bass.IndirectOffsetOnAxis(ap=slot[:, t, k:k + 1], axis=0),
                                in_=entry[:, t, k, :], in_offset=None).then_inc(s_slots, 16)


def mixer_phase(nc, sem, bank, cst, x_d, ctx_d, cst_d, par_d, wqkv_d, wo_d, inw_d, xpw_d,
                dtw_d, gate_d, bc_d, slots0_d, slots_d, xn_d, out_d, counts, slot, entry, s_slot, s_slots):
    with ExitStack() as st:
        def sb(name, shape, dt=F32):
            return st.enter_context(nc.sbuf_tensor(name, shape, dt))

        ident, rot, mask = cst[:, 0:P], cst[:, P:2 * P], cst[:, 2 * P:3 * P]
        cos, sin = cst[:, 3 * P:3 * P + S], cst[:, 3 * P + S:3 * P + 2 * S]
        tri = cst[:, 3 * P + 2 * S:4 * P + 2 * S]
        expert_no, part_no = cst[:, CST - E - 1:CST - 1], cst[:, CST - 1:CST]
        ones = sb("ones", [P, P])
        identb = sb("identb", [P, P], BF16)
        maskb = sb("maskb", [P, P], BF16)
        par = sb("par", [P, NE, PAR])
        conv_w = lambda e, k: par[:, e, k:k + 1]
        conv_b = lambda e: par[:, e, 4:5]
        dt_b = lambda e: par[:, e, 5:6]
        aneg = sb("aneg", [P, NE, DS])
        aexp = sb("aexp", [P, NE, DS])
        diagD = sb("diagD", [P, NE, P])
        wo = sb("wo", [P, NG, H])
        inw = sb("inw", [P, 2, DI])
        xpw = sb("xpw", [P, NE, DR + 2 * DS])
        dtw = sb("dtw", [DR, DI])
        gw = sb("gw", [P, NK, E])
        eps = sb("eps", [P, 1])

        xin0 = sb("xin0", [P, NT, H])
        xb = sb("xb", [P, NT, H])
        ctxT = sb("ctxT", [P, 2, S])
        ln = sb("ln", [P, NT, H])
        lnT = sb("lnT", [P, NK, S])
        nothing = sb("nothing", [P, 1])
        stats = sb("stats", [P, NT, 6])
        mv = sb("mv", [P, NT, 2])
        lnv = sb("lnv", [P, NT])
        r0 = sb("r0", [P, NT])
        nt1 = sb("nt1", [P, NT])
        nt2 = sb("nt2", [P, NT])
        nt3 = sb("nt3", [P, NT])
        rstd = sb("rstd", [P, NT])
        xin = sb("xin", [P, NE, S + DC - 1])
        u = sb("u", [P, NE, S])
        delta = sb("delta", [P, NE, S])
        du = sb("du", [P, NE, S])
        xdbl = sb("xdbl", [DR + 2 * DS, S])
        bcn = sb("bcn", [P, NSG, 2, S])
        dA = sb("dA", [P, 2, S])
        dBu2 = sb("dBu2", [P, 2, S])
        dBu = [dBu2[:, 0, :], dBu2[:, 1, :], ctxT[:, 0, :], ctxT[:, 1, :]]
        hst = sb("hst", [P, 2, S])

        wqkv = sb("wqkv", [P, NG, 3, NK, P])
        qwork = sb("qwork", [P, RING, S])
        qraw, qcos = qwork[:, 0:2, :], qwork[:, 2:4, :]
        hC = qwork
        qsin = sb("qsin", [P, 2, S])
        qkall = sb("qkall", [P, NG, 2, S])
        vall = sb("vall", [P, NG, NT, P])
        qk = sb("qk", [P, 2, S])
        vg = sb("vg", [P, NT, P])
        prob = sb("prob", [P, 2, S])
        probT = sb("probT", [P, 2, S])
        nmx = sb("nmx", [P, STEPS])
        rsum = sb("rsum", [P, STEPS])
        rinv = sb("rinv", [P, NG, STEPS])
        rrep = ln[:, :, :].rearrange("p g (t j d) -> p g t j d", t=NT, j=HG)
        ao = lnT

        gmx = sb("gmx", [P, NT])
        gexp = sb("gexp", [P, NT, E])
        gsum = sb("gsum", [P, NT])
        grec = sb("grec", [P, NT])
        prb = sb("prb", [P, NT, E + 2])
        top8 = sb("top8", [P, NT, 8])
        rest = sb("rest", [P, NT, E + 2])
        idx8 = sb("idx8", [P, NT, 8], mybir.dt.uint32)
        idxf = sb("idxf", [P, NT, 8])
        chosen = sb("chosen", [P, NT, E])
        before = sb("before", [P, NT + 1, E])
        rank = sb("rank", [P, NT, E])
        picked = sb("picked", [P, E])
        rk = sb("rk", [P, NT, TOPK])
        rki = sb("rki", [P, NT, TOPK], mybir.dt.int32)
        rlo = sb("rlo", [P, NT, TOPK], mybir.dt.int32)
        rhi = sb("rhi", [P, NT, TOPK], mybir.dt.int32)
        tokf = sb("tokf", [P, NT])

        Y = bank[0:4]
        S0, S1, TB, OB = bank[4:8]
        F4 = [S0, S1, TB, OB]

        s_const = sem("s_const")
        s_weights = sem("s_weights")
        s_load = sem("s_load")
        s_ctx = sem("s_ctx")
        s_bcst = sem("s_bcst")
        s_bc = [sem(f"s_bc{i}") for i in range(2)]
        s_setup_a = sem("s_setup_a")
        s_setup_p = sem("s_setup_p")
        s_setup_v = sem("s_setup_v")
        s_var = sem("s_var")
        s_lnv = sem("s_lnv")
        s_r0 = sem("s_r0")
        s_ln = sem("s_ln")
        s_lnTp = sem("s_lnTp")
        s_lnT = sem("s_lnT")
        s_xinp = sem("s_xinp")
        s_xin = sem("s_xin")
        s_conv = sem("s_conv")
        s_u = sem("s_u")
        s_xdp = sem("s_xdp")
        s_xd = sem("s_xd")
        s_dtp = sem("s_dtp")
        s_abs = sem("s_abs")
        s_relu = sem("s_relu")
        s_e = sem("s_e")
        s_l = sem("s_l")
        s_w1 = sem("s_w1")
        s_l2 = sem("s_l2")
        s_delta = sem("s_delta")
        s_du = sem("s_du")
        s_qp = sem("s_qp")
        s_qraw = sem("s_qraw")
        s_v = sem("s_v")
        s_rotp = sem("s_rotp")
        s_qcos = sem("s_qcos")
        s_qsin = sem("s_qsin")
        s_qk = sem("s_qk")
        s_sc = sem("s_sc")
        s_nmx = sem("s_nmx")
        s_prob = sem("s_prob")
        s_tp = sem("s_tp")
        s_pt = sem("s_pt")
        s_pv = sem("s_pv")
        s_dA = sem("s_dA")
        s_dBu = sem("s_dBu")
        s_scan = sem("s_scan")
        s_hC = sem("s_hC")
        s_pair = sem("s_pair")
        s_y = sem("s_y")
        s_rinv = sem("s_rinv")
        s_rrep = sem("s_rrep")
        s_rbp = sem("s_rbp")
        s_ob = sem("s_ob")
        s_qks = sem("s_qks")
        s_vs = sem("s_vs")
        s_ao = sem("s_ao")
        s_wop = sem("s_wop")
        s_att = sem("s_att")
        s_gate = sem("s_gate")
        s_yg = sem("s_yg")
        s_ytp = sem("s_ytp")
        s_x2 = sem("s_x2")
        s_xt = sem("s_xt")
        s_gp = sem("s_gp")
        s_gmx = sem("s_gmx")
        s_gexp = sem("s_gexp")
        s_chosen = sem("s_chosen")
        s_rankp = sem("s_rankp")
        s_counts = sem("s_counts")
        s_init = sem("s_init")
        s_carry = sem("s_carry")
        s_x2st = sem("s_x2st")
        s_small = sem("s_small")

        from_one = (s_att, s_qk, s_xt, s_x2st, s_bcst, s_tp, s_pv, s_gexp, s_yg, s_qcos, s_rotp, s_qraw, s_qsin, s_v, s_ao, s_ob,
                    s_sc, s_counts)

        with nc.Block() as block:

            @block.sync
            def _(sp):
                for one in from_one:
                    sp.sem_inc(one, 1)
                sp.sem_inc(s_y, SUMS)
                sp.sem_inc(s_pair, len(ADDED))

                def load_tokens(b):
                    sp.dma_start(xin0[:, :, :], x_d[bass.ds(b, 1), :, :, :].rearrange("a p t h -> (a p) t h")).then_inc(s_load, 16)

                def load_context(b):
                    sp.dma_start(ctxT[:, :, :], ctx_d[bass.ds(b, 1), :, :, :].rearrange("a p t h -> (a p) t h")).then_inc(s_ctx, 16)

                def states(b):
                    sp.wait_ge(s_xd, b + 1)
                    sp.dma_start(bc_d[bass.ds(b, 1), :, :].rearrange("a r s -> (a r) s"), xdbl[DR:DR + 2 * DS, :]).then_inc(s_bcst, 16)
                    with sp.Fori(0, NG) as g:
                        it = b * NG + g
                        sp.wait_ge(s_bcst, 1 + b * 16 + 16)
                        for p in range(NSG // 2):
                            sp.wait_ge(s_hC, it * STEPS + (p + 1) * 2 * NE)
                            for n in range(2 * p, 2 * p + 2):
                                for row in range(2):
                                    src = bc_d[bass.ds(b, 1), bass.ds(g * NSG + (row * DS + n), 1), :].rearrange("a r s -> (a r) s")
                                    sp.dma_start(bcn[:, n, row, :], src.to_broadcast([P, S])).then_inc(s_bc[p], 16)

                for dst, src in ((cst[:, :], cst_d[:, :]), (par[:, :, :], par_d[:, :, :]), (inw[:, :, :], inw_d[:, :, :])):
                    sp.dma_start(dst, src).then_inc(s_const, 16)
                load_context(0)
                load_tokens(0)
                for dst, src in ((wqkv[:, :, :, :, :], wqkv_d[:, :, :, :, :]), (xpw[:, :, :], xpw_d[:, :, :]), (dtw[:, :], dtw_d[:, :]),
                                 (wo[:, :, :], wo_d[:, :, :]), (gw[:, :, :], gate_d[:, :, :])):
                    sp.dma_start(dst, src).then_inc(s_weights, 16)
                sp.dma_start(xn_d[TOK:ROWS, :].rearrange("(t p) h -> p t h", p=P), x_d[0, :, 0:HALVES, :]).then_inc(s_init, 16)
                with sp.Fori(0, NB - 1) as b:
                    states(b)
                    sp.wait_ge(s_scan, (b * NG + NG) * STEPS + 4)
                    load_context(b + 1)
                    sp.wait_ge(s_att, 1 + b * NT + NT)
                    load_tokens(b + 1)
                states(NB - 1)
                sp.wait_ge(s_xt, 1 + NB * 16)
                sp.wait_ge(s_init, 16)
                sp.wait_ge(s_x2st, 1 + NB * 16)

            @block.gpsimd
            def _(pool):
                pool.dma_start(slots_d[:, :], slots0_d[:, :]).then_inc(s_slots, 16)
                pool.memset(xin[:, :, 0:DC - 1], 0.0).then_inc(s_setup_p, 1)
                pool.memset(eps[:, :], EPS).then_inc(s_setup_p, 1)
                pool.memset(ones[:, :], 1.0).then_inc(s_setup_p, 1)
                pool.memset(counts[:, :], 0.0).then_inc(s_setup_p, 1)
                pool.memset(before[:, 0, :], 0.0).then_inc(s_setup_p, 1)
                pool.memset(prb[:, :, E:E + 2], -1.0).then_inc(s_setup_p, 1)

                def times_cos(gi):
                    for c in range(2):
                        pool.wait_ge(s_qraw, 1 + gi * 2 + c + 1)
                        pool.wait_ge(s_qk, 1 + gi * 2)
                        pool.tensor_tensor(qcos[:, c, :], qraw[:, c, :], cos, ALU.mult).then_inc(s_qcos, 1)

                def add_pair(it, q):
                    pool.wait_ge(s_hC, it * STEPS + 2 * q + 2 + STEPS)
                    even, odd = 2 * q % RING, (2 * q + 1) % RING
                    pool.tensor_tensor(hC[:, odd, :], hC[:, even, :], hC[:, odd, :], ALU.add).then_inc(s_pair, 1)

                def scan_inputs(b):
                    times_cos(b * NG)
                    times_cos(b * NG + 1)
                    for e in range(NE):
                        pool.wait_ge(s_w1, b * 2 * NE + NE + e + 1)
                        pool.wait_ge(s_l, b * NE + e + 1)
                        pool.tensor_tensor(ln[:, e, :], ln[:, e, :], xin[:, e, DC - 1:], ALU.subtract).then_inc(s_l2, 1)
                    for e in range(NE):
                        pool.wait_ge(s_l2, b * NE + e + 1)
                        pool.wait_ge(s_relu, b * NE + e + 1)
                        pool.tensor_tensor(delta[:, e, :], delta[:, e, :], ln[:, e, :], ALU.add).then_inc(s_delta, 1)
                    times_cos(b * NG + 2)
                    times_cos(b * NG + 3)
                    with pool.Fori(0, NG) as g:
                        it = b * NG + g
                        for s in range(STEPS):
                            n, e = scan_step(s)
                            if s == 0:
                                pool.wait_ge(s_du, b * NE + NE)
                            if s % (2 * NE) == 0:
                                pool.wait_ge(s_bc[n // 2], it * 64 + 64)
                            pool.wait_ge(s_scan, it * STEPS + s + 1)
                            pool.tensor_tensor(dBu[s % 4], du[:, e, :], bcn[:, n, 0, :], ALU.mult).then_inc(s_dBu, 1)
                            if s % 2 == 0 and s // 2 - 2 in ADDED:
                                add_pair(it, s // 2 - 2)
                        if PAIRS - 2 in ADDED:
                            add_pair(it, PAIRS - 2)

                scan_inputs(0)
                with pool.Fori(1, NB) as b:
                    scan_inputs(b)
                    fill_slots(pool, b - 1, 0, NT * TOPK, slot, entry, s_slot, s_slots, s_carry, slots_d)

            @block.scalar
            def _(act):
                act.wait_ge(s_const, 16 * 3)
                act.wait_ge(s_setup_p, 6)
                act.activation(aexp[:, :, :], par[:, :, 7:PAR], ACT.Exp).then_inc(s_setup_a, 1)
                act.activation(identb[:, :], ident, ACT.Copy).then_inc(s_setup_a, 1)
                act.activation(maskb[:, :], mask, ACT.Copy).then_inc(s_setup_a, 1)

                def rstd_guess(i):
                    act.wait_ge(s_var, i + 1)
                    act.activation(lnv[:, :], mv[:, :, 1], ACT.Ln, bias=eps[:, 0:1]).then_inc(s_lnv, 1)
                    act.wait_ge(s_lnv, i + 1)
                    act.activation(r0[:, :], lnv[:, :], ACT.Exp, scale=-0.5).then_inc(s_r0, 1)

                def copy_lnT(i):
                    for k in range(NK):
                        act.wait_ge(s_lnTp, i * NK + k + 1)
                        act.activation(lnT[:, k, :], F4[k][:, :], ACT.Copy).then_inc(s_lnT, 1)

                def copy_qkv(gi, g):
                    for c in range(2):
                        act.wait_ge(s_qp, gi * 3 + c + 1)
                        act.wait_ge(s_qcos, 1 + gi * 2)
                        act.wait_ge(s_rotp, 1 + gi * 2)
                        act.activation(qraw[:, c, :], Y[c][:, :], ACT.Copy, scale=SCALE if c == 0 else 1.0).then_inc(s_qraw, 1)
                    act.wait_ge(s_qp, gi * 3 + 3)
                    act.activation(vall[:, g, :, :], Y[2][:, :].rearrange("p (t o) -> p t o", t=NT), ACT.Copy).then_inc(s_v, 1)

                def copy_context(b):
                    for e in range(NE):
                        act.wait_ge(s_xinp, b * NE + e + 1)
                        act.activation(xin[:, e, DC - 1:], F4[e][:, :], ACT.Copy).then_inc(s_xin, 1)

                def begin_mixing(b):
                    copy_lnT(b * 2)
                    for e in range(NE):
                        act.wait_ge(s_conv, b * NE * DC + NE * (DC - 1) + e + 1)
                        act.activation(u[:, e, :], du[:, e, :], ACT.Silu).then_inc(s_u, 1)
                    act.preload_act_table_set("natural_log_exp_and_others")
                    copy_qkv(b * NG, 0)
                    act.wait_ge(s_xdp, b + 1)
                    act.wait_ge(s_bcst, 1 + b * 16)
                    act.activation(xdbl[:, :], S0[0:DR + 2 * DS, :], ACT.Copy).then_inc(s_xd, 1)
                    copy_qkv(b * NG + 1, 1)

                def mix(b, more):
                    for e in range(NE):
                        act.wait_ge(s_dtp, b * NE + e + 1)
                        act.activation(ln[:, e, :], F4[e][:, :], ACT.Abs, bias=dt_b(e)).then_inc(s_abs, 1)
                    for e in range(NE):
                        act.wait_ge(s_abs, b * NE + e + 1)
                        act.activation(du[:, e, :], ln[:, e, :], ACT.Exp, scale=-1.0).then_inc(s_e, 1)
                    for e in range(NE):
                        act.wait_ge(s_e, b * NE + e + 1)
                        act.activation(ln[:, e, :], du[:, e, :], ACT.Ln, bias=1.0).then_inc(s_l, 1)
                    copy_qkv(b * NG + 2, 2)
                    copy_qkv(b * NG + 3, 3)

                    with act.Fori(0, NG) as g:
                        it = b * NG + g
                        def decay(s):
                            n, e = scan_step(s)
                            if s == 0:
                                act.wait_ge(s_delta, b * NE + NE)
                            act.wait_ge(s_scan, it * STEPS + s + 3)
                            act.activation(dA[:, s % 2, :], delta[:, e, :], ACT.Exp,
                                           scale=aneg[:, e, bass.ds(g * NSG + n, 1)]).then_inc(s_dA, 1)

                        def softmax(s):
                            w = (s % NT + 1) * P
                            act.wait_ge(s_nmx, it * STEPS + s + 1)
                            act.wait_ge(s_tp, 1 + it * STEPS + max(s - 1, 0))
                            act.activation(prob[:, s % 2, 0:w], [S0, S1][s % 2][:, 0:w], ACT.Exp, bias=nmx[:, s:s + 1],
                                           accum_out=rsum[:, s:s + 1]).then_inc(s_prob, 1)

                        def copy_probT(s):
                            w = (s % NT + 1) * P
                            act.wait_ge(s_tp, 1 + it * STEPS + s + 1)
                            act.wait_ge(s_pv, 1 + it * STEPS + max(s - 1, 0))
                            act.activation(probT[:, s % 2, 0:w], TB[:, 0:w], ACT.Copy).then_inc(s_pt, 1)

                        decay(0)
                        for k in range(STEPS + 1):
                            if k + 1 < STEPS:
                                decay(k + 1)
                            if k == 0:
                                act.wait_ge(s_pv, 1 + it * STEPS)
                                act.wait_ge(s_v, 1 + b * NG + NG)
                                act.activation(vg[:, :, :], vall[:, bass.ds(g, 1), :, :].rearrange("p a t o -> p (a t) o"),
                                               ACT.Copy).then_inc(s_vs, 1)
                            if k < STEPS:
                                softmax(k)
                            if k >= 1:
                                copy_probT(k - 1)
                        act.wait_ge(s_pv, 1 + it * STEPS + STEPS)
                        act.activation(ao[:, bass.ds(g, 1), :].rearrange("p a s -> p (a s)"), OB[:, :], ACT.Copy).then_inc(s_ob, 1)

                    rstd_guess(b * 3 + 1)
                    for t in range(NT):
                        act.wait_ge(s_ln, b * 3 * NT + NT + t + 1)
                        act.activation(delta[:, t, :], ln[:, t, :], ACT.Silu).then_inc(s_gate, 1)
                    if more:
                        copy_context(b + 1)
                    act.preload_act_table_set("natural_log_exp_and_others")
                    rstd_guess(b * 3 + 2)
                    act.wait_ge(s_ln, b * 3 * NT + 3 * NT)
                    act.dma_start(xn_d[bass.ds(b * S, S), :].rearrange("(t p) h -> p t h", p=P), ln[:, :, :]).then_inc(s_xt, 16)
                    act.dma_start(out_d[bass.ds(b * S, S), :].rearrange("(t p) h -> p t h", p=P), xb[:, :, :]).then_inc(s_x2st, 16)
                    copy_lnT(b * 2 + 1)
                    if more:
                        rstd_guess(b * 3 + 3)
                    for t in range(NT):
                        act.wait_ge(s_gmx, b + 1)
                        act.activation(gexp[:, t, :], Y[2][:, t * E:(t + 1) * E], ACT.Exp, bias=gmx[:, t:t + 1],
                                       accum_out=gsum[:, t:t + 1]).then_inc(s_gexp, 1)
                    if more:
                        begin_mixing(b + 1)

                act.preload_act_table_set("natural_log_exp_and_others")
                copy_context(0)
                rstd_guess(0)
                begin_mixing(0)
                with act.Fori(0, NB - 1) as b:
                    mix(b, True)
                mix(NB - 1, False)

            @block.vector
            def _(v):
                v.wait_ge(s_const, 16 * 3)
                v.wait_ge(s_setup_a, 3)
                v.tensor_scalar(aneg[:, :, :], aexp[:, :, :], -1.0, None, ALU.mult).then_inc(s_setup_v, 1)
                for e in range(NE):
                    v.tensor_scalar(diagD[:, e, :], ident, par[:, e, 6:7], None, ALU.mult).then_inc(s_setup_v, 1)
                for t in range(NT):
                    v.tensor_scalar(tokf[:, t:t + 1], part_no, float(t * P), None, ALU.add).then_inc(s_setup_v, 1)
                v.sem_inc(s_scan, 4)
                v.sem_inc(s_hC, STEPS)

                class Chain:
                    n = 0
                    base = 0

                def link(ins, own_wait=False):
                    Chain.n += 1
                    ins.then_inc(s_small, 1)
                    v.wait_ge(s_small, Chain.base + Chain.n)
                    if own_wait:
                        v.memset(nothing[:, :], 0.0)

                def row_stats(src, tiles):
                    for t in tiles:
                        ins = v.bn_stats(stats[:, t, :], src[:, t, :])
                    return ins

                def layer_norm(i, src, left=range(NT), free=None):
                    link(row_stats(src, left), own_wait=True)
                    for t in range(NT):
                        ins = v.bn_aggr(mv[:, t, :], stats[:, t, :])
                    ins.then_inc(s_var, 1)
                    v.wait_ge(s_r0, i + 1)
                    link(v.tensor_tensor(nt1[:, :], r0[:, :], r0[:, :], ALU.mult))
                    link(v.scalar_tensor_tensor(nt2[:, :], mv[:, :, 1], EPS, nt1[:, :], ALU.add, ALU.mult))
                    link(v.tensor_scalar(nt3[:, :], nt2[:, :], -0.5, 1.5, ALU.mult, ALU.add))
                    link(v.tensor_tensor(rstd[:, :], r0[:, :], nt3[:, :], ALU.mult))
                    if free:
                        free()
                    for t in range(NT):
                        v.tensor_scalar(ln[:, t, :], src[:, t, :], mv[:, t, 0:1], rstd[:, t:t + 1], ALU.subtract,
                                        ALU.mult).then_inc(s_ln, 1)

                def rotate(gi, g):
                    v.wait_ge(s_qk, 1 + gi * 2)
                    for c, src in ((0, Y[3]), (1, Y[1])):
                        v.wait_ge(s_rotp, 1 + gi * 2 + c + 1)
                        v.tensor_tensor(qsin[:, c, :], src[:, :], sin, ALU.mult).then_inc(s_qsin, 1)
                    for c in range(2):
                        v.wait_ge(s_qsin, 1 + gi * 2 + c + 1)
                        v.wait_ge(s_qcos, 1 + gi * 2 + c + 1)
                        v.tensor_tensor(qkall[:, g, c, :], qcos[:, c, :], qsin[:, c, :], ALU.add).then_inc(s_qk, 1)

                LINKS = 3 * 5 + 2 + 5 + NT + 1 + NT * TOPK + 3

                def first_norm(b):
                    v.wait_ge(s_load, b * 16 + 16)
                    layer_norm(b * 3, xin0, free=lambda: v.wait_ge(s_xt, 1 + b * 16))

                def convolve(b, taps):
                    for k in taps:
                        for e in range(NE):
                            n = b * NE * DC + NE * k + e
                            if k == 0:
                                v.wait_ge(s_xin, b * NE + e + 1)
                                v.tensor_scalar(du[:, e, :], xin[:, e, 0:S], conv_w(e, 0), conv_b(e), ALU.mult,
                                                ALU.add).then_inc(s_conv, 1)
                            else:
                                v.wait_ge(s_conv, n - NE + 1)
                                v.scalar_tensor_tensor(du[:, e, :], xin[:, e, k:k + S], conv_w(e, k), du[:, e, :],
                                                       ALU.mult, ALU.add).then_inc(s_conv, 1)

                def begin_mixing(b):
                    rotate(b * NG, 0)
                    rotate(b * NG + 1, 1)

                def step_sizes(b):
                    for e in range(NE):
                        v.wait_ge(s_abs, b * NE + NE)
                        v.tensor_scalar(delta[:, e, :], F4[e][:, :], dt_b(e), 0.0, ALU.add, ALU.max).then_inc(s_relu, 1)
                    for e in range(NE):
                        v.wait_ge(s_e, b * NE + e + 1)
                        v.tensor_scalar(xin[:, e, DC - 1:], du[:, e, :], 1.0, 1.0, ALU.add, ALU.subtract).then_inc(s_w1, 1)
                    for e in range(NE):
                        v.wait_ge(s_w1, b * 2 * NE + e + 1)
                        v.tensor_tensor(xin[:, e, DC - 1:], xin[:, e, DC - 1:], du[:, e, :], ALU.subtract).then_inc(s_w1, 1)

                def mix(b):
                    for e in range(NE):
                        v.wait_ge(s_l2, b * NE + e + 1)
                        v.wait_ge(s_delta, b * NE + e + 1)
                        v.tensor_tensor(du[:, e, :], delta[:, e, :], u[:, e, :], ALU.mult).then_inc(s_du, 1)
                    rotate(b * NG + 2, 2)
                    rotate(b * NG + 3, 3)


                    def take_group(it, g):
                        v.wait_ge(s_sc, 1 + it * STEPS)
                        v.tensor_copy(qk[:, :, :], qkall[:, bass.ds(g, 1), :, :].rearrange("p a c s -> p (a c) s")).then_inc(s_qks, 1)

                    v.wait_ge(s_qk, 1 + b * 2 * NG + 2 * NG)
                    take_group(b * NG, 0)
                    with v.Fori(0, NG) as g:
                        it = b * NG + g

                        def c_product(s):
                            n, _ = scan_step(s)
                            v.wait_ge(s_scan, it * STEPS + s + 5)
                            last = s - RING if s >= RING else max(range(s, STEPS, RING))
                            if last // 2 in ADDED and last % 2 == 0:
                                v.wait_ge(s_pair, it * len(ADDED) + pairs_added(last // 2) + (len(ADDED) if last < s else 0))
                            else:
                                v.wait_ge(s_y, it * SUMS + sums_made(last) + (SUMS if last < s else 0))
                            v.tensor_tensor(hC[:, s % RING, :], hst[:, s % 2, :], bcn[:, n, 1, :], ALU.mult).then_inc(s_hC, 1)

                        for s in range(STEPS):
                            w = (s % NT + 1) * P
                            v.wait_ge(s_sc, 1 + it * STEPS + s + 1)
                            v.tensor_reduce(nmx[:, s:s + 1], [S0, S1][s % 2][:, 0:w], AX.X, ALU.max, negate=True).then_inc(s_nmx, 1)
                            v.wait_ge(s_dA, it * STEPS + s + 1)
                            v.wait_ge(s_dBu, it * STEPS + s + 1)
                            v.wait_ge(s_hC, it * STEPS + s - 1 + STEPS)
                            v.tensor_tensor_scan(hst[:, s % 2, :], dA[:, s % 2, :], dBu[s % 4], 0.0, ALU.mult,
                                                 ALU.add).then_inc(s_scan, 1)
                            if s >= 1:
                                c_product(s - 1)
                        with v.If(g < NG - 1):
                            take_group(it + 1, nc.s_assert_within(g + 1, 1, NG - 1, skip_runtime_bounds_check_because='inside the If'))
                        c_product(STEPS - 1)

                        v.wait_ge(s_prob, it * STEPS + STEPS)
                        v.reciprocal(rinv[:, bass.ds(g, 1), :].rearrange("p a s -> p (a s)"), rsum[:, :]).then_inc(s_rinv, 1)

                    for g in range(NG):
                        v.wait_ge(s_rinv, b * NG + NG)
                        v.tensor_copy(rrep[:, g, :, :, :],
                                      rinv[:, g, :].rearrange("p (j t) -> p t j", t=NT).unsqueeze(3).to_broadcast([P, NT, HG, HD])
                                      ).then_inc(s_rrep, 1)
                    for g in range(NG):
                        v.wait_ge(s_rbp, b * NG + g + 1)
                        v.wait_ge(s_ob, 1 + b * NG + NG)
                        v.tensor_tensor(ao[:, g, :], F4[g][:, :], ao[:, g, :], ALU.mult).then_inc(s_ao, 1)
                    for t in range(NT):
                        v.wait_ge(s_wop, b * NT + t + 1)
                        v.wait_ge(s_x2st, 1 + b * 16)
                        v.tensor_tensor(xb[:, t, :], F4[t][:, :], xin0[:, t, :], ALU.add).then_inc(s_att, 1)
                        v.wait_ge(s_att, 1 + b * NT + t + 1)
                        if t < NT - 1:
                            row_stats(xb, [t])
                    layer_norm(b * 3 + 1, xb, left=[NT - 1])
                    for t in range(NT):
                        v.wait_ge(s_gate, b * NT + t + 1)
                        v.wait_ge(s_y, (b * NG + NG + 1) * SUMS)
                        v.tensor_tensor(u[:, t, :], delta[:, t, :], Y[t][:, :], ALU.mult).then_inc(s_yg, 1)
                    for t in range(NT):
                        v.wait_ge(s_ytp, b * NT + t + 1)
                        v.tensor_tensor(xb[:, t, :], F4[t][:, :], xb[:, t, :], ALU.add).then_inc(s_x2, 1)
                    v.wait_ge(s_x2, b * NT + NT)
                    layer_norm(b * 3 + 2, xb)

                def route(b):
                    v.wait_ge(s_gp, b * NT + NT)
                    v.tensor_reduce(gmx[:, :], Y[2][:, 0:NT * E].rearrange("p (t e) -> p t e", t=NT), AX.X, ALU.max,
                                    negate=True).then_inc(s_gmx, 1)

                def weights(b):
                    v.wait_ge(s_gexp, 1 + b * NT + NT)
                    link(v.reciprocal(grec[:, :], gsum[:, :]))
                    for t in range(NT):
                        ins = v.tensor_scalar(prb[:, t, 0:E], gexp[:, t, :], grec[:, t:t + 1], None, ALU.mult)
                    link(ins, own_wait=True)
                    for t in range(NT):
                        ins = v.max(top8[:, t, :], prb[:, t, 0:E])
                    link(ins, own_wait=True)
                    for t in range(NT):
                        ins = v.max_index(idx8[:, t, :], top8[:, t, :], prb[:, t, 0:E])
                    link(ins)

                def choose(b):
                    v.wait_ge(s_slots, 16 + b * NT * TOPK * 16)
                    v.tensor_copy(entry[:, :, :, 1].bitcast(F32), top8[:, :, 0:TOPK])
                    v.tensor_copy(entry[:, :, :, 0], tokf[:, :].unsqueeze(2).to_broadcast([P, NT, TOPK]))
                    v.tensor_copy(idxf[:, :, :], idx8[:, :, :])
                    link(v.memset(top8[:, :, TOPK:8], -1.0), own_wait=True)
                    for t in range(NT):
                        ins = v.match_replace(rest[:, t, :], top8[:, t, :], prb[:, t, :], -2.0)
                    link(ins)
                    v.tensor_scalar(tokf[:, :], tokf[:, :], float(S), None, ALU.add)
                    link(v.tensor_scalar(chosen[:, :, :], rest[:, :, 0:E], -1.5, None, ALU.is_lt))
                    for t in range(NT):
                        link(v.tensor_tensor(before[:, t + 1, :], before[:, t, :], chosen[:, t, :], ALU.add))
                    v.sem_inc(s_chosen, 1)

                def rank_all(b):
                    v.wait_ge(s_rankp, b + 1)
                    v.tensor_tensor(rank[:, :, :], S1[:, 0:NT * E].rearrange("p (t e) -> p t e", t=NT),
                                    counts[:, :].unsqueeze(1).to_broadcast([P, NT, E]), ALU.add)
                    link(v.memset(nothing[:, :], 0.0))
                    v.tensor_tensor(counts[:, :], S1[:, NT * E:NT * E + E], counts[:, :], ALU.add).then_inc(s_counts, 1)

                def place(b):
                    for t in range(NT):
                        for k in range(TOPK):
                            ins = v.scalar_tensor_tensor(picked[:, :], expert_no, idxf[:, t, k:k + 1], rank[:, t, :], ALU.is_equal,
                                                         ALU.mult, accum_out=rk[:, t, k:k + 1])
                            link(ins)
                    link(v.tensor_copy(rki[:, :, :], rk[:, :, :]))
                    v.tensor_scalar(rlo[:, :, :], rki[:, :, :], P - 1, NJ.bit_length() - 1, ALU.bitwise_and, ALU.logical_shift_left)
                    link(v.tensor_scalar(rhi[:, :, :], rki[:, :, :], P.bit_length() - 1, SH * TOK, ALU.logical_shift_right, ALU.bitwise_or))
                    link(v.tensor_tensor(rlo[:, :, :], rlo[:, :, :], rhi[:, :, :], ALU.bitwise_or))
                    v.scalar_tensor_tensor(slot[:, :, :], idxf[:, :, 0:TOPK], float(TOK), rlo[:, :, :], ALU.mult,
                                           ALU.add).then_inc(s_slot, 1)

                first_norm(0)
                convolve(0, range(DC))
                begin_mixing(0)
                step_sizes(0)
                first_links = Chain.n
                with v.Fori(0, NB - 1) as b:
                    Chain.n, Chain.base = 0, first_links + b * LINKS
                    mix(b)
                    first_norm(b + 1)
                    route(b)
                    convolve(b + 1, range(DC))
                    weights(b)
                    choose(b)
                    begin_mixing(b + 1)
                    rank_all(b)
                    step_sizes(b + 1)
                    place(b)
                    assert Chain.n == LINKS, Chain.n
                Chain.n, Chain.base = 0, first_links + (NB - 1) * LINKS
                mix(NB - 1)
                route(NB - 1)
                weights(NB - 1)
                choose(NB - 1)
                rank_all(NB - 1)
                place(NB - 1)

            @block.tensor
            def _(pe):
                pe.wait_ge(s_const, 16 * 3)
                pe.wait_ge(s_setup_v, 1 + NE)

                def transpose_ln(b, which):
                    for k in range(NK):
                        for t in range(NT):
                            if k == 0:
                                pe.wait_ge(s_ln, b * 3 * NT + which * NT + t + 1)
                            ins = pe.transpose(F4[k][:, t * P:(t + 1) * P], ln[:, t, k * P:(k + 1) * P], ident)
                        ins.then_inc(s_lnTp, 1)

                def project_qkv(gi, g):
                    pe.wait_ge(s_qraw, 1 + gi * 2)
                    for k in range(NK):
                        ins = pe.matmul(Y[0][:, :], wqkv[:, g, 0, k, :], lnT[:, k, :], start=(k == 0), stop=(k == NK - 1))
                    ins.then_inc(s_qp, 1)
                    pe.wait_ge(s_qsin, 1 + gi * 2)
                    for k in range(NK):
                        ins = pe.matmul(Y[1][:, :], wqkv[:, g, 1, k, :], lnT[:, k, :], start=(k == 0), stop=(k == NK - 1))
                    ins.then_inc(s_qp, 1)
                    pe.wait_ge(s_qraw, 1 + gi * 2 + 1)
                    pe.matmul(Y[3][:, :], rot, qraw[:, 0, :], start=True, stop=True).then_inc(s_rotp, 1)
                    pe.wait_ge(s_v, 1 + gi)
                    if g == 0:
                        pe.wait_ge(s_gexp, 1 + gi)
                    for t in range(NT):
                        for k in range(NK):
                            ins = pe.matmul(Y[2][:, t * P:(t + 1) * P], lnT[:, k, t * P:(t + 1) * P], wqkv[:, g, 2, k, :],
                                            start=(k == 0), stop=(k == NK - 1))
                    ins.then_inc(s_qp, 1)
                    pe.wait_ge(s_qraw, 1 + gi * 2 + 2)
                    pe.matmul(Y[1][:, :], rot, qraw[:, 1, :], start=True, stop=True).then_inc(s_rotp, 1)

                def project_context(b, ahead):
                    pe.wait_ge(s_ctx, (b + ahead) * 16 + 16)
                    for e in range(NE):
                        if ahead:
                            pe.wait_ge(s_att, 1 + b * NT + e + 1)
                        for k in range(2):
                            ins = pe.matmul(F4[e][:, :], inw[:, k, e * P:(e + 1) * P], ctxT[:, k, :], start=(k == 0),
                                            stop=(k == 1))
                        ins.then_inc(s_xinp, 1)

                def begin_mixing(b):
                    transpose_ln(b, 0)
                    pe.wait_ge(s_yg, 1 + b * NT)
                    pe.wait_ge(s_lnT, b * 2 * NK + NK)
                    project_qkv(b * NG, 0)
                    for e in range(NE):
                        pe.wait_ge(s_u, b * NE + e + 1)
                        ins = pe.matmul(S0[0:DR + 2 * DS, :], xpw[:, e, :], u[:, e, :], start=(e == 0), stop=(e == NE - 1))
                    ins.then_inc(s_xdp, 1)
                    project_qkv(b * NG + 1, 1)

                def step_sizes(b):
                    pe.wait_ge(s_xd, b + 1)
                    pe.wait_ge(s_counts, 1 + b)
                    for e in range(NE):
                        pe.matmul(F4[e][:, :], dtw[:, e * P:(e + 1) * P], xdbl[0:DR, :], start=True, stop=True).then_inc(s_dtp, 1)

                def mix(b, more):
                    project_qkv(b * NG + 2, 2)
                    project_qkv(b * NG + 3, 3)
                    pe.wait_ge(s_qsin, 1 + b * 2 * NG + 2 * NG)
                    pe.wait_ge(s_v, 1 + b * NG + NG)
                    for e in range(NE):
                        pe.matmul(Y[e][:, :], diagD[:, e, :], u[:, e, :], start=True, stop=False, skip_group_check=True)

                    def scores(it, s):
                        j, t = divmod(s, NT)
                        r = slice(j * HD, (j + 1) * HD)
                        if s == 0:
                            pe.wait_ge(s_qks, it + 1)
                        if s >= 2:
                            pe.wait_ge(s_prob, it * STEPS + s - 1)
                        dst = [S0, S1][s % 2]
                        w = (t + 1) * P
                        pe.matmul(dst[:, 0:w], qk[r, 0, t * P:w], qk[r, 1, 0:w], start=True, stop=False)
                        pe.matmul(dst[:, t * P:w], identb[:, :], maskb[:, :], start=False, stop=True).then_inc(s_sc, 1)

                    pe.wait_ge(s_relu, b * NE + NE)
                    scores(b * NG, 0)
                    with pe.Fori(0, NG) as g:
                        it = b * NG + g

                        def transposes(s):
                            t = s % NT
                            pe.wait_ge(s_prob, it * STEPS + s + 1)
                            if s > 0:
                                pe.wait_ge(s_pt, it * STEPS + s)
                            for k in range(t + 1):
                                ins = pe.transpose(TB[:, k * P:(k + 1) * P], prob[:, s % 2, k * P:(k + 1) * P], ident)
                            ins.then_inc(s_tp, 1)

                        def values(s):
                            j, t = divmod(s, NT)
                            pe.wait_ge(s_pt, it * STEPS + s + 1)
                            if s == 0:
                                pe.wait_ge(s_ob, 1 + it)
                                pe.wait_ge(s_vs, it + 1)
                            for k in range(t + 1):
                                ins = pe.matmul(OB[j * HD:(j + 1) * HD, t * P:(t + 1) * P], vg[:, k, j * HD:(j + 1) * HD],
                                                probT[:, s % 2, k * P:(k + 1) * P], start=(k == 0), stop=(k == t))
                            ins.then_inc(s_pv, 1)

                        def sum_states(q):
                            _, e = scan_step(2 * q)
                            for step in (2 * q + 1,) if q in ADDED else (2 * q, 2 * q + 1):
                                if q in ADDED:
                                    pe.wait_ge(s_pair, (it + 1) * len(ADDED) + pairs_added(q))
                                else:
                                    pe.wait_ge(s_hC, it * STEPS + step + 1 + STEPS)
                                pe.matmul(Y[e][:, :], ident, hC[:, step % RING, :], start=False, stop=False,
                                          skip_group_check=True).then_inc(s_y, 1)

                        for k in range(STEPS + 2):
                            if k + 1 < STEPS:
                                scores(it, k + 1)
                            if 1 <= k <= STEPS:
                                transposes(k - 1)
                            if k == STEPS:
                                with pe.If(g < NG - 1):
                                    scores(it + 1, 0)
                            if k >= 2:
                                values(k - 2)
                            if k >= 6 and k % 2 == 0:
                                sum_states(k // 2 - 3)
                        sum_states(PAIRS - 2)
                        sum_states(PAIRS - 1)

                    pe.wait_ge(s_ob, 1 + b * NG + NG)
                    for g in range(NG):
                        pe.wait_ge(s_rrep, b * NG + g + 1)
                        for t in range(NT):
                            ins = pe.matmul(F4[g][:, t * P:(t + 1) * P], rrep[:, g, t, :, :].rearrange("p j d -> p (j d)"), ident,
                                            start=True, stop=True)
                        ins.then_inc(s_rbp, 1)
                    pe.wait_ge(s_ao, 1 + b * NG + NG)
                    for t in range(NT):
                        for g in range(NG):
                            ins = pe.matmul(F4[t][:, :], ao[:, g, t * P:(t + 1) * P], wo[:, g, :], start=(g == 0),
                                            stop=(g == NG - 1))
                        ins.then_inc(s_wop, 1)

                    if more:
                        project_context(b, 1)
                    for t in range(NT):
                        if more:
                            pe.wait_ge(s_xin, b * NE + NE + t + 1)
                        else:
                            pe.wait_ge(s_att, 1 + b * NT + t + 1)
                        for e in range(NE):
                            pe.wait_ge(s_yg, 1 + b * NT + e + 1)
                            ins = pe.transpose(F4[t][:, e * P:(e + 1) * P], u[:, e, t * P:(t + 1) * P], ident)
                        ins.then_inc(s_ytp, 1)
                    pe.wait_ge(s_x2, b * NT + NT)
                    transpose_ln(b, 2)
                    pe.wait_ge(s_lnT, b * 2 * NK + 2 * NK)
                    for t in range(NT):
                        for k in range(NK):
                            ins = pe.matmul(Y[2][:, t * E:(t + 1) * E], lnT[:, k, t * P:(t + 1) * P], gw[:, k, :],
                                            start=(k == 0), stop=(k == NK - 1))
                        ins.then_inc(s_gp, 1)

                def ranks(b):
                    pe.wait_ge(s_chosen, b + 1)
                    pe.matmul(S1[:, 0:NT * E], tri, chosen[:, :, :].rearrange("p t e -> p (t e)"), start=True, stop=False)
                    pe.matmul(S1[:, 0:NT * E], ones[:, :], before[:, 0:NT, :].rearrange("p t e -> p (t e)"), start=False, stop=True)
                    pe.matmul(S1[:, NT * E:NT * E + E], ones[:, :], before[:, NT, :], start=True, stop=True).then_inc(s_rankp, 1)

                project_context(0, 0)
                pe.wait_ge(s_xin, NE)
                pe.wait_ge(s_weights, 16 * 5)
                begin_mixing(0)
                step_sizes(0)
                with pe.Fori(0, NB - 1) as b:
                    mix(b, True)
                    begin_mixing(b + 1)
                    ranks(b)
                    step_sizes(b + 1)
                mix(NB - 1, False)
                ranks(NB - 1)


def expert_phase(nc, sem, bank, cst, counts, slot, entry, s_slot, s_slots, slots_d, xn_d, w1_d, w2_d, out_d):
    with ExitStack() as st:
        def sb(name, shape, dt=F32):
            return st.enter_context(nc.sbuf_tensor(name, shape, dt))

        I32, U32 = mybir.dt.int32, mybir.dt.uint32
        ident = cst[:, 0:P]
        table = sb("table", [P, NX, NJ, 2], I32)
        blocks = sb("blocks", [P, NX])
        upto = sb("upto", [P, NX])
        every = sb("every", [P, NX])
        plan = sb("plan", [P, NX, 2], I32)
        raw1 = sb("raw1", [P, NK, 2 * I])
        raw2 = sb("raw2", [P, 3, H])
        w1h = [sb(f"w1h{i}", [P, NK, 2 * I], F32R) for i in range(2)]
        w1l = [sb(f"w1l{i}", [P, NK, 2 * I], F32R) for i in range(2)]
        w2h = [sb(f"w2h{i}", [P, 3, H], F32R) for i in range(2)]
        w2l = [sb(f"w2l{i}", [P, 3, H], F32R) for i in range(2)]
        gidx = sb("gidx", [P, HALVES], U32)
        gone1 = sb("gone1", [P, HALVES], U32)
        gone2 = sb("gone2", [P, HALVES], U32)
        xg = [sb(f"xg{i}", [P, H]) for i in range(HALVES)]
        xh = sb("xh", [P, NK, BLK], F32R)
        xl = sb("xl", [P, NK, BLK], F32R)
        silu = sb("silu", [P, 3, BLK])
        a = sb("a", [P, 3, BLK])
        ah = sb("ah", [P, 3, BLK], F32R)
        al = sb("al", [P, 3, BLK], F32R)
        y = [sb(f"y{i}", [P, H]) for i in range(HALVES)]
        XT = bank[0:2]
        GU = bank[2:5]
        DOWN = bank[5:7]

        s_zero = sem("s_zero")
        s_shared = sem("s_shared")
        s_table = sem("s_table")
        s_plan = sem("s_plan")
        s_link = sem("s_link")
        s_raw = sem("s_raw")
        s_hi = sem("s_whi")
        s_lo = sem("s_wlo")
        s_gidx = sem("s_gidx")
        s_xg = sem("s_xg")
        s_xt = sem("s_xtp")
        s_xh = sem("s_xh")
        s_xl = sem("s_xl")
        s_up = sem("s_up")
        s_silu = sem("s_silu")
        s_a = sem("s_a")
        s_ah = sem("s_ah")
        s_al = sem("s_al")
        s_dn = sem("s_dn")
        s_y = [sem(f"s_y{i}") for i in range(HALVES)]
        s_gone1 = sem("s_gone1")
        s_gone2 = sem("s_gone2")
        s_out = sem("s_out")
        s_carry2 = sem("s_carry2")
        from_one = (s_lo, s_hi, s_xt, s_xh, s_xl, s_a, s_ah, s_al, s_dn, *s_y)

        def rows(c):
            return CH[c][1]

        HI_AT = ((0, 1), (2,), (3, 4), ())
        LO_AT = ((0,), (1,), (2,), (3, 4))

        def over_experts(eng, first, head, rest, tail, unroll=False):
            def expert(x, par, nxt):
                last = eng.value_load(plan[0:1, bass.ds(x, 1), 0], min_val=0, max_val=NBLK - 1)
                start = eng.value_load(plan[0:1, bass.ds(x, 1), 1], min_val=0, max_val=NX * NBLK)
                head(x, par, start, nxt)
                with eng.Fori(1, NBLK // 2) as j:
                    with eng.If(j <= last):
                        rest(x, par, start + j, start + (j - 1), j)
                with eng.If(last >= NBLK // 2):
                    with eng.Fori(NBLK // 2, NBLK) as j:
                        with eng.If(j <= last):
                            rest(x, par, start + j, start + (j - 1), j)
                tail(x, par, start + (last + 1), start + last, last, nxt)

            first()
            for x in range(SH):
                head(x, x, x * NBLK, True)
                if unroll:
                    for j in range(1, NBLK):
                        rest(x, x, x * NBLK + j, x * NBLK + j - 1, j)
                else:
                    with eng.Fori(1, NBLK) as j:
                        rest(x, x, x * NBLK + j, x * NBLK + (j - 1), j)
                if x == SH - 1:
                    eng.wait_ge(s_table, 16)
                tail(x, x, (x + 1) * NBLK, (x + 1) * NBLK - 1, NBLK - 1, True)
            eng.wait_ge(s_plan, 1)
            with eng.Fori(SH // 2, NX // 2 - 1) as pair:
                expert(pair * 2, 0, True)
                expert(pair * 2 + 1, 1, True)
            expert(NX - 2, 0, True)
            expert(NX - 1, 1, False)

        with nc.Block() as block:

            @block.sync
            def _(sp):
                for one in from_one:
                    sp.sem_inc(one, 1)
                sp.dma_start(table[:, 0:SH, :, :].rearrange("p x j c -> p x (j c)"),
                             slots_d[0:SH * TOK, :].rearrange("(x p j) c -> p x (j c)", p=P, j=NJ)).then_inc(s_shared, 16)
                sp.wait_ge(s_zero, 3)
                with sp.Fori(0, NX) as x:
                    sp.wait_ge(s_lo, 1 + x * (NK + 1))
                    sp.dma_start(raw1[:, :, :], w1_d[bass.ds(x, 1), :, :, :].rearrange("a p k o -> (a p) k o")).then_inc(s_raw, 16)
                    w2x = w2_d[bass.ds(x, 1), :, :].rearrange("a i h -> (a i) h")
                    sp.dma_start(raw2[:, 0:2, :], w2x[0:2 * P, :].rearrange("(c p) h -> p c h", p=P)).then_inc(s_raw, 16)
                    sp.dma_start(raw2[0:I - 2 * P, 2, :], w2x[2 * P:I, :]).then_inc(s_raw, 16)

            @block.gpsimd
            def _(pool):
                for i in range(2 * HALVES):
                    part = slice(TOK + i * (P // 2), TOK + (i + 1) * (P // 2))
                    pool.dma_start(out_d[part, :], xn_d[part, :]).then_inc(s_out, 16)
                pool.memset(raw2[:, 2, :], 0.0).then_inc(s_zero, 1)
                pool.memset(gidx[:, :], 0).then_inc(s_zero, 1)
                pool.memset(gone1[:, :], 0).then_inc(s_zero, 1)

                def gather(x, n, j):
                    pool.wait_ge(s_xt, 1 + n)
                    pool.sem_inc(s_carry2, 1)
                    if not (isinstance(n, int) and n < 3):
                        pool.wait_ge(s_out, n * HALVES * 16)
                        pool.sem_inc(s_carry2, 1)
                    if not (isinstance(n, int) and n == 0):
                        pool.tensor_copy(gone2[:, :], gone1[:, :]).then_inc(s_gone2, 1)
                        pool.wait_ge(s_gone2, n)
                        pool.sem_inc(s_carry2, 1)
                        pool.tensor_copy(gone1[:, :], gidx[:, :]).then_inc(s_gone1, 1)
                        pool.wait_ge(s_gone1, n)
                        pool.sem_inc(s_carry2, 1)
                    pool.tensor_copy(gidx[:, :], table[:, bass.ds(x, 1), bass.ds(j * HALVES, HALVES), 0].rearrange("p a j -> p (a j)")
                                     ).then_inc(s_gidx, 1)
                    pool.wait_ge(s_gidx, n + 1)
                    pool.sem_inc(s_carry2, 1)
                    for i in range(HALVES):
                        pool.indirect_dma_start(out=xg[i][:, :], out_offset=None, in_=xn_d[:, :],
                                                in_offset=bass.IndirectOffsetOnAxis(ap=gidx[:, i:i + 1], axis=0)).then_inc(s_xg, 16)

                def scatter(n, tokens):
                    pool.wait_ge(s_out, n * HALVES * 16)
                    pool.sem_inc(s_carry2, 1)
                    for i in range(HALVES):
                        pool.wait_ge(s_y[i], n)
                        pool.sem_inc(s_carry2, 1)
                        pool.indirect_dma_start(out=out_d[:, :], out_offset=bass.IndirectOffsetOnAxis(ap=tokens[:, i:i + 1], axis=0),
                                                in_=y[i][:, :], in_offset=None, bounds_check=ROWS - 1, compute_op=ALU.add).then_inc(s_out, 16)

                def first():
                    pool.wait_ge(s_shared, 16)
                    pool.wait_ge(s_zero, 3)
                    gather(0, 0, 0)

                def head(x, par, n, nxt):
                    if isinstance(x, int) and x == SH - 1:
                        pool.wait_ge(s_slots, 16 + NB * NT * TOPK * 16)
                        pool.dma_start(table[:, SH:NX, :, :].rearrange("p x j c -> p x (j c)"),
                                       slots_d[SH * TOK:NX * TOK, :].rearrange("(x p j) c -> p x (j c)", p=P, j=NJ)).then_inc(s_table, 16)

                def rest(x, par, n, before, j):
                    gather(x, n, j)
                    if isinstance(x, int) and x == 0:
                        fills = NT * TOPK // (NBLK - 2)
                        if j <= NBLK - 2:
                            fill_slots(pool, NB - 1, (j - 1) * fills, j * fills, slot, entry, s_slot, s_slots, s_carry2, slots_d)
                    if not (isinstance(n, int) and n < 2):
                        scatter(n, gone2)

                def tail(x, par, n, before, last, nxt):
                    if nxt:
                        gather(x + 1, n, 0)
                        scatter(n, gone2)
                    else:
                        scatter(n, gone1)
                        scatter(n + 1, gidx)

                over_experts(pool, first, head, rest, tail, unroll=True)
                total = pool.value_load(plan[0:1, NX - 1:NX, 0], min_val=0, max_val=NBLK - 1) + \
                    pool.value_load(plan[0:1, NX - 1:NX, 1], min_val=0, max_val=NX * NBLK) + 1
                pool.wait_ge(s_out, (total + 2) * HALVES * 16)
                pool.sem_inc(s_carry2, 1)

            @block.scalar
            def _(act):
                def split_hi(x, par, n, k):
                    if k == 0:
                        act.wait_ge(s_raw, x * 48 + 48)
                        act.wait_ge(s_dn, 1 + n * HALVES)
                        act.activation(w2h[par][:, :, :], raw2[:, :, :], ACT.Copy).then_inc(s_hi, 1)
                    else:
                        act.activation(w1h[par][:, k - 1, :], raw1[:, k - 1, :], ACT.Copy).then_inc(s_hi, 1)

                def tokens(n):
                    act.wait_ge(s_xt, 1 + n + 1)
                    for i in range(2):
                        act.activation(xh[:, 2 * i:2 * i + 2, :], XT[i][:, :].rearrange("p (k s) -> p k s", k=2), ACT.Copy).then_inc(s_xh, 1)

                def hidden(n, between=lambda c: None):
                    for c in range(3):
                        between(c)
                        m = rows(c)
                        act.wait_ge(s_up, n * 3 + c + 1)
                        act.activation(silu[0:m, c, :], GU[c][0:m, 0:BLK], ACT.Silu).then_inc(s_silu, 1)
                        act.wait_ge(s_a, 1 + n * 3 + c + 1)
                        act.activation(ah[0:m, c, :], a[0:m, c, :], ACT.Copy).then_inc(s_ah, 1)
                    between(3)

                def weigh(x, n, j):
                    act.wait_ge(s_dn, 1 + n * HALVES + 2)
                    act.wait_ge(s_out, (n + 2) * HALVES * 16)
                    act.activation(y[1][:, :], DOWN[1][:, :], ACT.Copy,
                                   scale=table[:, bass.ds(x, 1), bass.ds(j * HALVES + 1, 1), 1].rearrange("p a j -> p (a j)").bitcast(F32)
                                   ).then_inc(s_y[1], 1)

                def first():
                    for k in range(NK + 1):
                        split_hi(0, 0, 0, k)
                    act.wait_ge(s_shared, 16)
                    tokens(0)

                def head(x, par, n, nxt):
                    hidden(n, lambda c: [split_hi(x + 1, 1 - par, n, k) for k in HI_AT[c] if nxt])

                def rest(x, par, n, before, j):
                    tokens(n)
                    weigh(x, before, j - 1)
                    hidden(n)

                def tail(x, par, n, before, last, nxt):
                    if nxt:
                        tokens(n)
                    weigh(x, before, last)

                act.preload_act_table_set("silu_and_others")
                over_experts(act, first, head, rest, tail)

            @block.vector
            def _(v):
                links = 0

                def link(ins):
                    nonlocal links
                    links += 1
                    ins.then_inc(s_link, 1)
                    v.wait_ge(s_link, links)

                v.memset(every[:, :], 1.0)
                link(v.memset(blocks[:, :], 1.0))
                for j in range(1, NBLK):
                    link(v.scalar_tensor_tensor(blocks[:, SH:NX], counts[:, :], float(j * BLK), blocks[:, SH:NX], ALU.is_gt, ALU.add))
                link(v.memset(blocks[:, 0:SH], float(NBLK)))
                link(v.tensor_tensor_scan(upto[:, :], every[:, :], blocks[:, :], 0.0, ALU.mult, ALU.add))
                v.tensor_scalar(plan[:, :, 0], blocks[:, :], 1.0, None, ALU.subtract)
                v.tensor_tensor(plan[:, :, 1], upto[:, :], blocks[:, :], ALU.subtract).then_inc(s_plan, 1)

                def split_lo(x, par, k):
                    v.wait_ge(s_hi, 1 + x * (NK + 1) + k + 1)
                    if k == 0:
                        v.tensor_tensor(w2l[par][:, :, :], raw2[:, :, :], w2h[par][:, :, :].bitcast(F32), ALU.subtract).then_inc(s_lo, 1)
                    else:
                        v.tensor_tensor(w1l[par][:, k - 1, :], raw1[:, k - 1, :], w1h[par][:, k - 1, :].bitcast(F32),
                                        ALU.subtract).then_inc(s_lo, 1)

                def tokens(n):
                    v.wait_ge(s_xh, 1 + n * 2 + 2)
                    for i in range(2):
                        v.tensor_tensor(xl[:, 2 * i:2 * i + 2, :], XT[i][:, :].rearrange("p (k s) -> p k s", k=2),
                                        xh[:, 2 * i:2 * i + 2, :].bitcast(F32), ALU.subtract).then_inc(s_xl, 1)

                def hidden(n, between=lambda c: None):
                    for c in range(3):
                        between(c)
                        m = rows(c)
                        v.wait_ge(s_silu, n * 3 + c + 1)
                        v.tensor_tensor(a[0:m, c, :], GU[c][0:m, BLK:2 * BLK], silu[0:m, c, :], ALU.mult).then_inc(s_a, 1)
                        v.wait_ge(s_ah, 1 + n * 3 + c + 1)
                        v.tensor_tensor(al[0:m, c, :], a[0:m, c, :], ah[0:m, c, :].bitcast(F32), ALU.subtract).then_inc(s_al, 1)
                    between(3)

                def weigh(x, n, j):
                    v.wait_ge(s_dn, 1 + n * HALVES + 1)
                    v.wait_ge(s_out, (n + 2) * HALVES * 16)
                    v.tensor_scalar(y[0][:, :], DOWN[0][:, :],
                                    table[:, bass.ds(x, 1), bass.ds(j * HALVES, 1), 1].rearrange("p a j -> p (a j)").bitcast(F32),
                                    None, ALU.mult).then_inc(s_y[0], 1)

                def first():
                    for k in range(NK + 1):
                        split_lo(0, 0, k)
                    v.wait_ge(s_shared, 16)
                    tokens(0)

                def head(x, par, n, nxt):
                    hidden(n, lambda c: [split_lo(x + 1, 1 - par, k) for k in LO_AT[c] if nxt])

                def rest(x, par, n, before, j):
                    tokens(n)
                    weigh(x, before, j - 1)
                    hidden(n)

                def tail(x, par, n, before, last, nxt):
                    if nxt:
                        tokens(n)
                    weigh(x, before, last)

                over_experts(v, first, head, rest, tail)

            @block.tensor
            def _(pe):
                def tokens(n):
                    pe.wait_ge(s_xg, (n + 1) * HALVES * 16)
                    pe.wait_ge(s_xl, 1 + n * 2)
                    for k in range(NK):
                        for i in range(HALVES):
                            ins = pe.transpose(XT[k // 2][:, (k % 2) * BLK + i * P:(k % 2) * BLK + (i + 1) * P],
                                               xg[i][:, k * P:(k + 1) * P], ident)
                    ins.then_inc(s_xt, 1)

                def gate_up(par, n):
                    pe.wait_ge(s_xl, 1 + n * 2 + 2)
                    pe.wait_ge(s_a, 1 + n * 3)
                    for c, (o, m) in enumerate(CH):
                        for dst, off in ((GU[c][0:m, 0:BLK], 0), (GU[c][0:m, BLK:2 * BLK], I)):
                            i = 0
                            for wp, xp in ((w1h, xh), (w1h, xl), (w1l, xh)):
                                for k in range(NK):
                                    ins = pe.matmul(dst, wp[par][:, k, off + o:off + o + m], xp[:, k, :],
                                                    start=(i == 0), stop=(i == 3 * NK - 1))
                                    i += 1
                        ins.then_inc(s_up, 1)

                def down(par, n):
                    for t in range(HALVES):
                        pe.wait_ge(s_y[t], 1 + n)
                        for c in range(3):
                            pe.wait_ge(s_al, 1 + n * 3 + c + 1)
                            m = rows(c)
                            for j, (ap, wp) in enumerate(((ah, w2h), (ah, w2l), (al, w2h))):
                                ins = pe.matmul(DOWN[t][:, :], ap[0:m, c, t * P:(t + 1) * P], wp[par][0:m, c, :],
                                                start=(c == 0 and j == 0), stop=(c == 2 and j == 2))
                        ins.then_inc(s_dn, 1)

                def first():
                    tokens(0)

                def head(x, par, n, nxt):
                    pe.wait_ge(s_lo, 1 + (x + 1) * (NK + 1))
                    gate_up(par, n)

                def rest(x, par, n, before, j):
                    tokens(n)
                    down(par, before)
                    gate_up(par, n)

                def tail(x, par, n, before, last, nxt):
                    if nxt:
                        tokens(n)
                    down(par, before)

                over_experts(pe, first, head, rest, tail)


def kernel(**inputs):
    import numpy as np
    import concourse.bacc as bacc
    from concourse import mybir as mb
    from concourse.bass_utils import run_bass_kernel_spmd

    def rope():
        inv = 1.0 / 10000.0 ** (np.arange(0, HD, 2, dtype=np.float32) / HD)
        freqs = np.einsum("i,j->ij", np.arange(S, dtype=np.float32), inv)
        emb = np.concatenate((freqs, freqs), axis=-1)
        rot = np.zeros((P, P), np.float32)
        for h in range(HG):
            for d in range(HD // 2):
                rot[h * HD + HD // 2 + d, h * HD + d] = -1.0
                rot[h * HD + d, h * HD + HD // 2 + d] = 1.0
        return np.tile(np.cos(emb).T, (HG, 1)), np.tile(np.sin(emb).T, (HG, 1)), rot

    cos, sin, rot = rope()
    mask = np.where(np.arange(P)[None, :] > np.arange(P)[:, None], np.float32(-1e30), np.float32(0))
    tri = np.triu(np.ones((P, P), np.float32), 1)
    numbers = np.concatenate([np.tile(np.arange(E), (P, 1)), np.arange(P)[:, None]], axis=1)
    cst = np.concatenate([np.eye(P), rot, mask, cos, sin, tri, numbers], axis=1).astype(np.float32)

    slots = np.zeros((NX, P, NJ, 2), np.int32)
    slots[..., 0] = TOK + np.arange(P)[:, None] + P * (np.arange(NJ) % HALVES)
    slots[:SH, :, :, 0] = np.arange(P)[:, None] + P * np.arange(NJ)
    slots[:SH, :, :, 1] = np.ones((), np.float32).view(np.int32)

    g = {k: np.asarray(v) for k, v in inputs.items()}
    par = np.concatenate([g["L0_xattn_conv_w"], g["L0_xattn_conv_b"][:, None], g["L0_xattn_dt_proj_b"][:, None],
                          g["L0_xattn_D"][:, None], g["L0_xattn_A_log"]], axis=1)

    def chunks(w):
        return w.reshape(w.shape[0] // P, P, w.shape[1]).transpose(1, 0, 2)

    qkv = np.stack([chunks(g["L0_attn_W" + c].T) for c in "qkv"], axis=1)
    qkv = qkv.reshape(P, 3, NK, NG, P).transpose(0, 3, 1, 2, 4)
    sw1 = g["L0_ffn_shared_w1"].reshape(2, 2, I, H).transpose(1, 0, 2, 3).reshape(2, 2 * I, H)
    w1 = np.concatenate([sw1, g["L0_ffn_w1"]]).transpose(0, 2, 1).reshape(NX, NK, P, 2 * I).transpose(0, 2, 1, 3)
    sw2 = g["L0_ffn_shared_w2"].T.reshape(2, I, H)
    w2 = np.concatenate([sw2, g["L0_ffn_w2"].transpose(0, 2, 1)])
    arrays = {
        "x": g["x"].reshape(NB, NT, P, H).transpose(0, 2, 1, 3),
        "ctx": g["ctx_1024"].transpose(0, 2, 1).reshape(NB, 2, P, S).transpose(0, 2, 1, 3),
        "cst": cst,
        "par": par.reshape(NE, P, PAR).transpose(1, 0, 2),
        "wqkv": qkv,
        "wo": chunks(g["L0_attn_Wo"].T),
        "inw": chunks(g["L0_xattn_in_proj_w"].T),
        "xpw": chunks(g["L0_xattn_x_proj_w"].T),
        "dtw": g["L0_xattn_dt_proj_w"].T,
        "gate": chunks(g["L0_ffn_gate_w"].T),
        "slots": slots.reshape(-1, 2),
        "w1": w1,
        "w2": w2,
    }
    arrays = {f"in_{k}": np.ascontiguousarray(v) for k, v in arrays.items()}
    nc = bacc.Bacc("TRN2", target_bir_lowering=False, num_devices=1)
    aps = {k: nc.dram_tensor(k, v.shape, mb.dt.from_np(v.dtype), kind="ExternalInput").ap() for k, v in arrays.items()}
    bc = nc.dram_tensor("bc_scratch", (NB, 2 * DS, S), mb.dt.float32, kind="Internal").ap()
    slots_d = nc.dram_tensor("slots_scratch", (NX * TOK, 2), mb.dt.int32, kind="Internal").ap()
    xn = nc.dram_tensor("xn_scratch", (ROWS, H), mb.dt.float32, kind="Internal").ap()
    out = nc.dram_tensor("out_0", (ROWS, H), mb.dt.float32, kind="ExternalOutput").ap()
    build(nc, *[aps["in_" + k] for k in ("x", "ctx", "cst", "par", "wqkv", "wo", "inw", "xpw", "dtw", "gate", "w1", "w2")],
          bc, aps["in_slots"], slots_d, xn, out)
    r = run_bass_kernel_spmd(nc, [arrays], core_ids=[0])
    return r.results[0]["out_0"][:TOK].reshape(NB, S, H)
```
